# Optimizing a Trainium2 kernel written in Bass

```python
import numpy as np
import jax
import jax.numpy as jnp

def _softmax(x, axis=-1):
    return jax.nn.softmax(x, axis=axis)

def _gelu(x):
    return jax.nn.gelu(x, approximate=True)

def _silu(x):
    return jax.nn.silu(x)

def _sigmoid(x):
    return jax.nn.sigmoid(x)

def _layernorm(x, axis=-1, eps=1e-05):
    m = jnp.mean(x, axis=axis, keepdims=True)
    v = jnp.var(x, axis=axis, keepdims=True)
    return (x - m) / jnp.sqrt(v + eps)

def _scatter_add(tgt, idx, src, axis=0):
    return tgt.at[idx].add(src)

def _segment_sum(src, seg, n):
    return jax.ops.segment_sum(src, seg, n)
kernel_name = 'mk_adaln_ffn_d2_seqx_r8_9b0f8c'

def setup_inputs(seed: int=0):
    np.random.seed(seed)
    _w = jnp.asarray

    def _rec_inputs():
        import jax
        import jax.numpy as jnp
        _rk = jax.random.key(seed)
        x = -0.000125 + 0.9999 * jax.random.normal(jax.random.fold_in(_rk, 1), (64, 32, 512), jnp.float32)
        _lenS = 32 - jax.random.randint(jax.random.fold_in(_rk, 7), (64,), 0, max(1, 32 // 4) + 1, jnp.int32)
        _lenS2 = 32 - jax.random.randint(jax.random.fold_in(_rk, 8), (64,), 0, max(1, 32 // 4) + 1, jnp.int32)
        cond_128 = 0.0061147 + 1.02565 * jax.random.normal(jax.random.fold_in(_rk, 11), (64, 128), jnp.float32)
        fside_S_0 = -0.022604 + 0.987366 * jax.random.normal(jax.random.fold_in(_rk, 12), (32,), jnp.float32)
        return (x, cond_128, fside_S_0)
    x, cond_128, fside_S_0 = _rec_inputs()

    def _L0_cond_setup():
        import jax, jax.numpy as jnp
        import numpy as np
        K = 8
        T = 1.0
        D_EMBD = 128
        IN_C = 32
        OUT_C = 32
        BS = 32
        H = 512
        HID = 128
        key = jax.random.key(seed)
        ks = jax.random.split(key, 10)
        s = lambda fan_in: 1.0 / np.sqrt(fan_in)
        return {'x': jax.random.normal(ks[0], (BS, IN_C, H), dtype=jnp.float32), 'embedding': jax.random.normal(ks[1], (BS, D_EMBD), dtype=jnp.float32), 'W0': jax.random.normal(ks[2], (D_EMBD, HID), dtype=jnp.float32) * s(D_EMBD), 'b0': jnp.zeros((HID,), dtype=jnp.float32), 'W1': jax.random.normal(ks[3], (HID, HID), dtype=jnp.float32) * s(HID), 'b1': jnp.zeros((HID,), dtype=jnp.float32), 'W2': jax.random.normal(ks[4], (HID, K), dtype=jnp.float32) * s(HID), 'b2': jnp.zeros((K,), dtype=jnp.float32), 'weight': jax.random.normal(ks[5], (K, OUT_C, IN_C, 1), dtype=jnp.float32) * s(IN_C), 'bias_k': jax.random.normal(ks[6], (K, OUT_C), dtype=jnp.float32) * 0.1}
    _L0_cond_all = _L0_cond_setup()
    _L0_cond_in = {k: v for k, v in _L0_cond_all.items() if k in ('W0', 'b0', 'W1', 'b1', 'W2', 'b2', 'weight', 'bias_k')}
    del _L0_cond_all

    def _L0_ffn_setup():
        import jax, jax.numpy as jnp
        import numpy as np
        GROUP_SIZE = 128

        def dequantize(imatrix, scales, zeros, group_size, out_dtype):
            rs = jnp.repeat(scales, group_size, axis=0)
            rz = jnp.repeat(zeros, group_size, axis=0)
            return ((imatrix.astype(rs.dtype) - rz.astype(rs.dtype)) * rs).astype(out_dtype)
        key = jax.random.key(seed)
        ks = jax.random.split(key, 10)
        H, I, G = (512, 1792, GROUP_SIZE)
        B, S = (4, 256)
        x = jax.random.normal(ks[0], (B, S, H), dtype=jnp.float32)
        gate_w = jax.random.randint(ks[1], (H, I), 0, 16, dtype=jnp.int32)
        gate_z = jax.random.randint(ks[2], (H // G, I), 0, 16, dtype=jnp.int32)
        gate_s = jax.random.uniform(ks[3], (H // G, I), dtype=jnp.float32) * 0.01
        up_w = jax.random.randint(ks[4], (H, I), 0, 16, dtype=jnp.int32)
        up_z = jax.random.randint(ks[5], (H // G, I), 0, 16, dtype=jnp.int32)
        up_s = jax.random.uniform(ks[6], (H // G, I), dtype=jnp.float32) * 0.01
        down_w = jax.random.randint(ks[7], (I, H), 0, 16, dtype=jnp.int32)
        down_z = jax.random.randint(ks[8], (I // G, H), 0, 16, dtype=jnp.int32)
        down_s = jax.random.uniform(ks[9], (I // G, H), dtype=jnp.float32) * 0.01
        return {'x': x, 'gate_w': gate_w, 'gate_z': gate_z, 'gate_s': gate_s, 'up_w': up_w, 'up_z': up_z, 'up_s': up_s, 'down_w': down_w, 'down_z': down_z, 'down_s': down_s}
    _L0_ffn_all = _L0_ffn_setup()
    _L0_ffn_in = {k: v for k, v in _L0_ffn_all.items() if k in ('gate_w', 'gate_z', 'gate_s', 'up_w', 'up_z', 'up_s', 'down_w', 'down_z', 'down_s')}
    del _L0_ffn_all

    def _L1_cond_setup():
        import jax, jax.numpy as jnp
        import numpy as np
        from jax import lax
        N, C_IN, L = (32, 32, 512)
        C_OUT, K, GROUPS = (32, 9, 4)
        C_DIM, PAD, STRIDE = (128, 4, 1)
        key = jax.random.key(seed)
        k1, k2, k3, k4, k5 = jax.random.split(key, 5)
        x = jax.random.normal(k1, (N, C_IN, L), dtype=jnp.float32)
        c = jax.random.normal(k2, (N, C_DIM), dtype=jnp.float32)
        weight = jax.random.normal(k3, (C_OUT, C_IN // GROUPS, K), dtype=jnp.float32)
        c_weight = jax.random.normal(k4, (C_OUT, C_DIM), dtype=jnp.float32)
        bias = jax.random.normal(k5, (C_OUT,), dtype=jnp.float32)
        return {'x': x, 'c': c, 'weight': weight, 'c_weight': c_weight, 'bias': bias}
    _L1_cond_all = _L1_cond_setup()
    _L1_cond_in = {k: v for k, v in _L1_cond_all.items() if k in ('weight', 'c_weight')}
    del _L1_cond_all

    def _L1_ffn_setup():
        import jax, jax.numpy as jnp
        import numpy as np
        B, T, D_IN, D_OUT = (8, 256, 512, 512)
        N_LORAS, RANK = (16, 32)
        SCALING = 1.0
        key = jax.random.key(seed)
        ks = jax.random.split(key, 8)
        std = 1.0 / D_IN ** 0.5
        x = jax.random.normal(ks[0], (B, T, D_IN), dtype=jnp.float32)
        idx = jax.random.randint(ks[1], (B,), 0, N_LORAS)
        gate = jax.nn.one_hot(idx, N_LORAS, dtype=jnp.float32)
        kernel = jax.random.normal(ks[2], (D_IN, D_OUT), dtype=jnp.float32) * std
        bias = jnp.zeros((D_OUT,), dtype=jnp.float32)
        lora_A = jax.random.normal(ks[3], (N_LORAS, RANK, D_IN), dtype=jnp.float32) * std
        lora_B = jax.random.normal(ks[4], (N_LORAS, D_OUT, RANK), dtype=jnp.float32) * 0.01
        lora_A_shared = jax.random.normal(ks[5], (RANK, D_IN), dtype=jnp.float32) * std
        lora_B_shared = jax.random.normal(ks[6], (D_OUT, RANK), dtype=jnp.float32) * 0.01
        return {'x': x, 'gate': gate, 'kernel': kernel, 'bias': bias, 'lora_A': lora_A, 'lora_B': lora_B, 'lora_A_shared': lora_A_shared, 'lora_B_shared': lora_B_shared}
    _L1_ffn_all = _L1_ffn_setup()
    _L1_ffn_in = {k: v for k, v in _L1_ffn_all.items() if k in ('gate', 'kernel', 'bias', 'lora_A', 'lora_B', 'lora_A_shared', 'lora_B_shared')}
    del _L1_ffn_all
    return {'x': x, 'cond_128': cond_128, 'fside_S_0': fside_S_0, 'L0_cond_W0': _L0_cond_in['W0'], 'L0_cond_b0': _L0_cond_in['b0'], 'L0_cond_W1': _L0_cond_in['W1'], 'L0_cond_b1': _L0_cond_in['b1'], 'L0_cond_W2': _L0_cond_in['W2'], 'L0_cond_b2': _L0_cond_in['b2'], 'L0_cond_weight': _L0_cond_in['weight'], 'L0_cond_bias_k': _L0_cond_in['bias_k'], 'L0_ffn_gate_w': _L0_ffn_in['gate_w'], 'L0_ffn_gate_z': _L0_ffn_in['gate_z'], 'L0_ffn_gate_s': _L0_ffn_in['gate_s'], 'L0_ffn_up_w': _L0_ffn_in['up_w'], 'L0_ffn_up_z': _L0_ffn_in['up_z'], 'L0_ffn_up_s': _L0_ffn_in['up_s'], 'L0_ffn_down_w': _L0_ffn_in['down_w'], 'L0_ffn_down_z': _L0_ffn_in['down_z'], 'L0_ffn_down_s': _L0_ffn_in['down_s'], 'L1_cond_weight': _L1_cond_in['weight'], 'L1_cond_c_weight': _L1_cond_in['c_weight'], 'L1_ffn_gate': _L1_ffn_in['gate'], 'L1_ffn_kernel': _L1_ffn_in['kernel'], 'L1_ffn_bias': _L1_ffn_in['bias'], 'L1_ffn_lora_A': _L1_ffn_in['lora_A'], 'L1_ffn_lora_B': _L1_ffn_in['lora_B'], 'L1_ffn_lora_A_shared': _L1_ffn_in['lora_A_shared'], 'L1_ffn_lora_B_shared': _L1_ffn_in['lora_B_shared']}

def reference(x, cond_128, fside_S_0, L0_cond_W0, L0_cond_b0, L0_cond_W1, L0_cond_b1, L0_cond_W2, L0_cond_b2, L0_cond_weight, L0_cond_bias_k, L0_ffn_gate_w, L0_ffn_gate_z, L0_ffn_gate_s, L0_ffn_up_w, L0_ffn_up_z, L0_ffn_up_s, L0_ffn_down_w, L0_ffn_down_z, L0_ffn_down_s, L1_cond_weight, L1_cond_c_weight, L1_ffn_gate, L1_ffn_kernel, L1_ffn_bias, L1_ffn_lora_A, L1_ffn_lora_B, L1_ffn_lora_A_shared, L1_ffn_lora_B_shared):
    import jax
    import jax.numpy as jnp

    def _L0_cond_ref(x, embedding, W0, b0, W1, b1, W2, b2, weight, bias_k):
        import jax, jax.numpy as jnp
        import numpy as np
        K = 8
        T = 1.0
        D_EMBD = 128
        IN_C = 32
        OUT_C = 32
        BS = 32
        H = 512
        HID = 128
        h = jax.nn.gelu(embedding @ W0 + b0, approximate=False)
        h = jax.nn.gelu(h @ W1 + b1, approximate=False)
        att = jax.nn.softmax((h @ W2 + b2) / T, axis=-1)
        agg_w = jnp.einsum('bk,koi->boi', att, weight[..., 0])
        agg_b = att @ bias_k
        out = jnp.einsum('boi,bih->boh', agg_w, x) + agg_b[:, :, None]
        return out

    def _L0_ffn_ref(x, gate_w, gate_z, gate_s, up_w, up_z, up_s, down_w, down_z, down_s):
        import jax, jax.numpy as jnp
        import numpy as np
        GROUP_SIZE = 128

        def dequantize(imatrix, scales, zeros, group_size, out_dtype):
            rs = jnp.repeat(scales, group_size, axis=0)
            rz = jnp.repeat(zeros, group_size, axis=0)
            return ((imatrix.astype(rs.dtype) - rz.astype(rs.dtype)) * rs).astype(out_dtype)
        dt = x.dtype
        gate_proj = dequantize(gate_w, gate_s, gate_z, GROUP_SIZE, dt)
        up_proj = dequantize(up_w, up_s, up_z, GROUP_SIZE, dt)
        down_proj = dequantize(down_w, down_s, down_z, GROUP_SIZE, dt)
        gate = jax.nn.silu(jnp.dot(x, gate_proj))
        up = jnp.dot(x, up_proj)
        return jnp.dot(gate * up, down_proj)

    def _L1_cond_ref(x, c, weight, c_weight, bias):
        import jax, jax.numpy as jnp
        import numpy as np
        from jax import lax
        N, C_IN, L = (32, 32, 512)
        C_OUT, K, GROUPS = (32, 9, 4)
        C_DIM, PAD, STRIDE = (128, 4, 1)
        out = lax.conv_general_dilated(x, weight, window_strides=(STRIDE,), padding=[(PAD, PAD)], dimension_numbers=('NCH', 'OIH', 'NCH'), feature_group_count=GROUPS)
        ctx = jnp.einsum('nd,od->no', c, c_weight)
        out = out + ctx[:, :, None] + bias[None, :, None]
        return out

    def _L1_ffn_ref(x, gate, kernel, bias, lora_A, lora_B, lora_A_shared, lora_B_shared):
        import jax, jax.numpy as jnp
        import numpy as np
        B, T, D_IN, D_OUT = (8, 256, 512, 512)
        N_LORAS, RANK = (16, 32)
        SCALING = 1.0
        base_out = jnp.matmul(x, kernel) + bias
        b = gate.shape[0]
        x_flat = x.reshape(b, -1, x.shape[-1])
        A_eff = jnp.einsum('bn,nri->bri', gate, lora_A)
        B_eff = jnp.einsum('bn,nor->bor', gate, lora_B)
        Ax = jnp.einsum('bri,bti->btr', A_eff, x_flat)
        delta_flat = jnp.einsum('bor,btr->bto', B_eff, Ax)
        Ax_s = jnp.einsum('ri,bti->btr', lora_A_shared, x_flat)
        delta_flat = delta_flat + jnp.einsum('or,btr->bto', lora_B_shared, Ax_s)
        delta = delta_flat.reshape(x.shape[:-1] + (kernel.shape[-1],))
        return base_out + (SCALING * delta).astype(base_out.dtype)
    x = x + _L0_ffn_ref(_L0_cond_ref(x, cond_128, L0_cond_W0, L0_cond_b0, L0_cond_W1, L0_cond_b1, L0_cond_W2, L0_cond_b2, L0_cond_weight, L0_cond_bias_k), L0_ffn_gate_w, L0_ffn_gate_z, L0_ffn_gate_s, L0_ffn_up_w, L0_ffn_up_z, L0_ffn_up_s, L0_ffn_down_w, L0_ffn_down_z, L0_ffn_down_s)
    x = x + _L1_ffn_ref(_L1_cond_ref(x, cond_128, L1_cond_weight, L1_cond_c_weight, fside_S_0), L1_ffn_gate, L1_ffn_kernel, L1_ffn_bias, L1_ffn_lora_A, L1_ffn_lora_B, L1_ffn_lora_A_shared, L1_ffn_lora_B_shared)
    return x

_drawn_inputs = setup_inputs


def setup_inputs(seed=0):
    import zlib

    import numpy as np

    out = dict(_drawn_inputs(seed))
    spreads = {'L0_cond_b0': (0.0, 0.8),
     'L0_cond_b1': (0.0, 0.8),
     'L0_cond_b2': (0.0, 0.746),
     'L1_ffn_bias': (0.0, 0.8)}
    factors = {}
    for name, (base, spread) in spreads.items():
        noise = np.random.default_rng([zlib.crc32(name.encode()), seed]).standard_normal(out[name].shape)
        drawn = base * np.exp(spread * noise) if base else spread * noise
        out[name] = jnp.asarray(drawn.astype(out[name].dtype))
    for name, factor in factors.items():
        out[name] = (out[name] * factor).astype(out[name].dtype)
    return out
```

```python
from contextlib import ExitStack

import concourse.bass as bass
from concourse import mybir

F32 = mybir.dt.float32
F32R = mybir.dt.float32r
I32 = mybir.dt.int32
ALU = mybir.AluOpType
ACT = mybir.ActivationFunctionType
AX = mybir.AxisListType

P = 128
B, S, H = 64, 32, 512
I = 1792
G = H // P
IT = I // P
TOK = 512
TB = B * S // TOK
BB = TOK // S
UNITS = TB * IT
PH = 4
C = H // P
KX = 8
NL, R = 16, 32
GB = 8
QB = 4
NQ = B // QB
BANKS = 8
DOWN_AFTER = 1
MIX_AT = 8

START = dict(w0=128, w1=128, w2=KX, emb=B, cw=128, b0=1, b1=1, fside=1, b2=KX, conv=3 * 128)
KEEP = dict(ident=128, delta=32, wmix=2 * 32, gate=4 * GB, sgu=IT * 2 * G, sd=C * IT, bias=C, bk=32, sha=PH * R)


def spans(widths):
    at, out = 0, {}
    for name, w in widths.items():
        out[name] = (at, at + w)
        at += w
    return out, at


START_AT, START_W = spans(START)
KEEP_AT, KEEP_W = spans(KEEP)


def ring_order():
    out = []

    def add(engine, *tile):
        out.append((tile, engine))

    def codes(it):
        for kind in range(3):
            add("dve", "zero", it, kind)

    codes(0)
    add("act", "hid", 0)
    add("act", "hid", 1)
    add("act", "logit")
    add("dve", "ctx")
    add("dve", "att")
    add("dve", "agg", 0)
    for c in range(G):
        add("dve", "mix", 0, c)
    for u in range(UNITS + 1):
        tb, it = divmod(u, IT)
        seq = []
        if u < UNITS:
            for g in range(G):
                seq.append(("act" if g == 0 else "dve", "gate", u, g))
                seq.append(("act" if g == 0 else "dve", "up", u, g))
        if u >= 1:
            down = [("act", "down", u - 1, c) for c in range(C)]
            if seq:
                seq = seq[:6] + down[:1] + seq[6:7] + down[1:2] + seq[7:] + down[2:]
            else:
                seq = down
        if u + 1 < IT:
            for kind, at in ((0, 2), (1, 5), (2, 8)):
                seq.insert(at, ("dve", "zero", u + 1, kind))
        out += [(x[1:], x[0]) for x in seq]
        if u < UNITS and tb + 1 < TB:
            if it == MIX_AT:
                add("dve", "agg", tb + 1)
            if MIX_AT < it <= MIX_AT + G:
                add("dve", "mix", tb + 1, it - MIX_AT - 1)
    add("dve", "turn", 0)
    for q in range(NQ + 5):
        if q + 1 < NQ:
            add("dve", "turn", q + 1)
        if q < NQ:
            add("dve", "conv", q)
        if 1 <= q <= NQ:
            add("dve", "back", q - 1)
        if 1 <= q <= 2:
            add("dve", "lora_a", 2 * q - 2)
            add("dve", "lora_a", 2 * q - 1)
            add("dve", "lora_b", q - 1)
        if q >= 4 and q % 4 == 0 and q // 4 <= TB:
            add("dve", "ax", q // 4 - 1)
        if q >= 5 and (q - 5) // 4 < TB:
            add("dve", "lin", (q - 5) // 4, (q - 5) % 4)
    return out


def ffn_block_kernel(nc, start, keep, codes, zeros, x_rows, x_phase, k_raw, lora_a, lora_b, shared_b, out):
    ring = ring_order()
    place = {tile: n for n, (tile, _) in enumerate(ring)}
    turns = {"act": 0, "dve": 0}
    freed_at = []
    for _, engine in ring:
        turns[engine] += 1
        freed_at.append((engine, turns[engine]))

    with ExitStack() as ctx:
        def sb(name, shape, dt=F32):
            return ctx.enter_context(nc.sbuf_tensor(name, shape, dt))

        def sem(name):
            return ctx.enter_context(nc.semaphore(name))

        psum = ctx.enter_context(nc.psum_tensor("psum", [P, BANKS, 512], F32))

        wgu = sb("wgu", [P, IT * 2 * G * P], F32R)
        wd = sb("wd", [P, IT * C * P], F32R)
        mixed = sb("mixed", [P, 2, 2, G * TOK], F32R)
        hid = sb("hid", [P, 2, 2, TOK], F32R)
        resid = sb("resid", [P, B, PH, S])
        acc = sb("acc", [P, 2, 2, TOK])
        part = sb("part", [P, 3, TOK])
        blocks = sb("blocks", [P, BB // 4, P])
        load = sb("load", [P, 6144])
        abf = sb("abf", [KX, TOK])
        abr = sb("abr", [64, TOK], F32R)
        convw = sb("convw", [P, 2, 3 * P], F32R)
        kc = sb("kc", [P, KEEP_W])
        onesr = sb("onesr", [64, P], F32R)
        identr = sb("identr", [3 * IT, 3 * IT], F32R)
        ones = sb("ones", [1, B])
        attrep = sb("attrep", [P, 2, B])
        att_t = sb("att_t", [KX, B])
        ctxb = sb("ctxb", [P, B])
        soft = sb("soft", [B, 4 + KX])

        def kept(name, rows=P):
            a, b = KEEP_AT[name]
            return kc[0:rows, a:b]

        wgu_v = wgu[:, :].rearrange("p (t k g i) -> p t k g i", t=IT, k=2, g=G)
        wd_v = wd[:, :].rearrange("p (t c m) -> p t c m", t=IT, c=C)
        mixed_v = mixed[:, :, :, :].rearrange("p b h (g t) -> p b h g t", g=G)
        sgu = kept("sgu").rearrange("p (t k g) -> p t k g", t=IT, k=2)
        sd = kept("sd").rearrange("p (c t) -> p c t", c=C)
        ident = kept("ident")
        acc_f = acc[:, :, :, :].rearrange("p a b t -> p (a b t)")

        def first(name, rows=P):
            a, b = START_AT[name]
            return acc_f[0:rows, a:b]
        att_wide = acc_f[0:B, 1024:1280]
        zeros_i = acc_f[0:3 * IT, 1280:1792].bitcast(I32)
        hid_t = acc_f[:, 1792:1920].rearrange("p (n b) -> p n b", n=2)
        zeros_r = wgu_v[0:3 * IT, IT - 1, 1, :, :].rearrange("p g i -> p (g i)")
        stage = load[:, 0:3072].rearrange("p (s n) -> p s n", s=2)
        xrow = load[:, 3072:5120].rearrange("p (t h) -> p t h", t=4)
        chooser = load[:, 5120:6144].rearrange("p (k n) -> p k n", k=2)
        k_f = load[:, 0:2048]
        la_f = load[:, 2048:4096].rearrange("p (k n) -> p k n", k=4)
        lb_f = load[:, 4096:6144].rearrange("p (k n) -> p k n", k=4)
        shb_f = blocks[64:96, :, :].rearrange("p a b -> p (a b)")
        kr = wgu[:, 0:4096].rearrange("p (h k c m) -> p h k c m", h=2, k=PH, c=C)
        ar = wgu[:, 4096:7168].rearrange("p (h k t r) -> p h k t r", h=2, k=PH, t=TB)
        br = wgu[0:96, 7168:11264].rearrange("p (h t c m) -> p h t c m", h=2, t=TB, c=C)
        cin = wd[:, 0:2 * 2 * QB * 130].rearrange("p (s h b m) -> p s h b m", s=2, h=2, b=QB)
        cout = acc_f[:, 0:1024].rearrange("p (s b m) -> p s b m", s=2, b=QB)
        gsel = acc_f[:, 1024:2048].rearrange("p (k n) -> p k n", k=4)
        lin_in = mixed[:, :, :, :].rearrange("p s h (b k o) -> p s h b k o", b=BB, k=PH)
        axr = hid[0:96, :, :, :]
        staged = part

        start_in, keep_in, zeros_in = sem("start_in"), sem("keep_in"), sem("zeros_in")
        codes_in = [sem("codes_in0"), sem("codes_in1")]
        rows_in = sem("rows_in")
        resid_in = [sem(f"resid_in{t}") for t in range(TB)]
        k_in, la_in, lb_in, shb_in = sem("k_in"), sem("la_in"), sem("lb_in"), sem("shb_in")
        stored = [sem(f"stored{i}") for i in range(3)]
        filled = sem("filled")
        freed = {"act": sem("freed_act"), "dve": sem("freed_dve")}
        memsets = sem("memsets")
        zeros_ready = sem("zeros_ready")
        hid_ready = sem("hid_ready")
        negmax_ready, exp_ready = sem("negmax_ready"), sem("exp_ready")
        dve_chain = sem("dve_chain")
        att_ready = sem("att_ready")
        chooser_ready = sem("chooser_ready")
        ab_hi, ab_lo = sem("ab_hi"), sem("ab_lo")
        conv_hi, conv_lo = sem("conv_hi"), sem("conv_lo")
        mix_hi = sem("mix_hi")
        silu_done, prod_done, hid_hi, hid_lo = sem("silu_done"), sem("prod_done"), sem("hid_hi"), sem("hid_lo")
        added = sem("added")
        k_hi, k_lo = sem("k_hi"), sem("k_lo")
        pads = sem("pads")
        turn_hi, back_hi, la_hi, lb_hi, ax_hi = (sem("turn_hi"), sem("back_hi"), sem("la_hi"),
                                                 sem("lb_hi"), sem("ax_hi"))
        sh_hi, sh_lo = sem("sh_hi"), sem("sh_lo")
        gsel_ready = sem("gsel_ready")

        def bank(*tile):
            return psum[:, place[tile] % BANKS, :]

        def is_filled(eng, *tile):
            eng.wait_ge(filled, place[tile] + 1)

        def is_freed(eng, *tile):
            engine, count = freed_at[place[tile]]
            eng.wait_ge(freed[engine], count)

        block = ctx.enter_context(nc.Block())

        @block.sync
        def _(sp):
            def load_codes(it):
                if it >= 2:
                    is_freed(sp, "zero", it - 2, 2)
                sp.dma_start(stage[:, it % 2, :].bitcast(I32), codes[it]).then_inc(codes_in[it % 2], 16)

            def load_rows(tb):
                if tb:
                    sp.wait_ge(filled, place[("mix", tb - 1, G - 1)] + 1)
                sp.dma_start(xrow, x_rows[tb]).then_inc(rows_in, 16)

            sp.dma_start(zeros_i, zeros).then_inc(zeros_in, 16)
            load_codes(0)
            load_rows(0)
            load_codes(1)
            sp.dma_start(resid[:, 0:BB, :, :], x_phase[:, 0:BB]).then_inc(resid_in[0], 16)
            for it in range(2, IT):
                load_codes(it)
                if it == 3:
                    load_rows(1)
            for tb in range(1, TB):
                sp.dma_start(resid[:, tb * BB:(tb + 1) * BB, :, :],
                             x_phase[:, tb * BB:(tb + 1) * BB]).then_inc(resid_in[tb], 16)
            for tb in range(2, TB):
                load_rows(tb)
            sp.wait_ge(filled, place[("mix", TB - 1, G - 1)] + 1)
            is_freed(sp, "agg", TB - 1)
            sp.dma_start(k_f, k_raw).then_inc(k_in, 16)
            sp.dma_start(la_f, lora_a).then_inc(la_in, 16)
            sp.dma_start(lb_f, lora_b).then_inc(lb_in, 16)
            sp.dma_start(shb_f, shared_b).then_inc(shb_in, 16)
            for n in range(TB * C):
                tb, c = divmod(n, C)
                is_freed(sp, "lin", tb, c)
                sp.dma_start(out[tb, c], staged[:, n % 3, :]).then_inc(stored[n % 3], 16)
            for s in range(3):
                sp.wait_ge(stored[s], 16 * len(range(s, TB * C, 3)))

        @block.tensor
        def _(pe):
            def claim(*tile):
                n = place[tile]
                if n >= BANKS:
                    engine, count = freed_at[n - BANKS]
                    pe.wait_ge(freed[engine], count)
                return psum[:, n % BANKS, :]

            def spread_zeros(it, kind):
                t = claim("zero", it, kind)
                r = kind * IT + it
                pe.matmul(t, identr[:, r:r + 1].to_broadcast([3 * IT, P]), zeros_r,
                          start=True, stop=True).then_inc(filled, 1)

            def aggregate(tb):
                t = claim("agg", tb)
                pe.wait_ge(chooser_ready, tb + 1)
                for n in range(4):
                    for k in range(2):
                        last = pe.matmul(t[:, n * S:(n + 1) * S], chooser[:, k, n * P:(n + 1) * P],
                                         kept("wmix").rearrange("p (k o) -> p k o", k=2)[:, k, :],
                                         start=(k == 0), stop=(k == 1))
                last.then_inc(filled, 1)

            def mix(tb, c):
                t = claim("mix", tb, c)
                if c == 0:
                    pe.wait_ge(rows_in, 16 * (tb + 1))
                    pe.wait_ge(ab_lo, tb + 1)
                    is_freed(pe, "agg", tb)
                pe.matmul(t, onesr[:, :], abr[:, :], start=True, stop=False)
                for n in range(4):
                    last = pe.matmul(t[:, n * P:(n + 1) * P], xrow[:, n, c * P:(c + 1) * P],
                                     blocks[:, n, :], start=False, stop=(n == 3))
                last.then_inc(filled, 1)

            def project(u, kind, g):
                tb, it = divmod(u, IT)
                t = claim(("gate", "up")[kind], u, g)
                if it == 0 and kind == 0:
                    is_freed(pe, "mix", tb, g)
                if tb == 0 and g == 0:
                    is_freed(pe, "zero", it, kind)
                for half in range(2):
                    last = pe.matmul(t, wgu_v[:, it, kind, g, :], mixed_v[:, tb % 2, half, g, :],
                                     start=(half == 0), stop=(half == 1))
                last.then_inc(filled, 1)

            def down(u, c):
                it = u % IT
                t = claim("down", u, c)
                if c == 0:
                    pe.wait_ge(hid_lo, u + 1)
                    if u < IT:
                        is_freed(pe, "zero", it, 2)
                for half in range(2):
                    last = pe.matmul(t, wd_v[:, it, c, :], hid[:, u % 2, half, :],
                                     start=(half == 0), stop=(half == 1))
                last.then_inc(filled, 1)

            def turn(q):
                t = claim("turn", q)
                tb = q * QB // BB
                pe.wait_ge(added, (tb + 1) * IT * C)
                for j in range(QB):
                    last = pe.transpose(t[:, j * P:(j + 1) * P],
                                        resid[:, q * QB + j, :, :].rearrange("p k o -> p (k o)"), ident)
                last.then_inc(filled, 1)

            def convolve(q):
                t = claim("conv", q)
                if q == 0:
                    pe.wait_ge(conv_lo, 1)
                is_freed(pe, "turn", q)
                n = 0
                for j in range(3):
                    for w, x in ((0, 0), (0, 1), (1, 0)):
                        last = pe.matmul(t, convw[:, w, j * P:(j + 1) * P], cin[:, q % 2, x, :, j:j + P],
                                         start=(n == 0), stop=(n == 8))
                        n += 1
                last.then_inc(filled, 1)

            def turn_back(q):
                t = claim("back", q)
                is_freed(pe, "conv", q)
                for j in range(QB):
                    last = pe.transpose(t[:, j * P:(j + 1) * P], cout[:, q % 2, j, :], ident)
                last.then_inc(filled, 1)

            def gate_a(k):
                t = claim("lora_a", k)
                if k == 0:
                    pe.wait_ge(gsel_ready, 1)
                    pe.wait_ge(la_in, 16)
                for n in range(4):
                    last = pe.matmul(t[:, 0:GB * R], la_f[:, n, k * P:(k + 1) * P], gsel[:, n, :],
                                     start=(n == 0), stop=(n == 3))
                last.then_inc(filled, 1)

            def gate_b(half):
                t = claim("lora_b", half)
                if half == 0:
                    pe.wait_ge(lb_in, 16)
                for n in range(4):
                    last = pe.matmul(t, gsel[:, n, half * P:(half + 1) * P], lb_f[:, n, :],
                                     start=(n == 0), stop=(n == 3))
                last.then_inc(filled, 1)

            THREE = ((0, 0), (0, 1), (1, 0))

            def lora_down(tb):
                t = claim("ax", tb)
                is_freed(pe, "back", 4 * tb + 3)
                if tb == 0:
                    is_freed(pe, "lora_a", PH - 1)
                    pe.wait_ge(sh_lo, 1)
                n = 0
                for k in range(PH):
                    for w, x in THREE:
                        last = pe.matmul(t[0:96, :], ar[:, w, k, tb, :], lin_in[:, tb % 2, x, :, k, :],
                                         start=(n == 0), stop=(n == 11))
                        n += 1
                last.then_inc(filled, 1)

            def linear(tb, c):
                t = claim("lin", tb, c)
                if tb == 0 and c == 0:
                    pe.wait_ge(k_lo, 1)
                    is_freed(pe, "lora_b", 1)
                    pe.wait_ge(sh_lo, 2)
                n = 0
                for k in range(PH):
                    for w, x in THREE:
                        pe.matmul(t, kr[:, w, k, c, :], lin_in[:, tb % 2, x, :, k, :],
                                  start=(n == 0), stop=False)
                        n += 1
                if c == 0:
                    is_freed(pe, "ax", tb)
                for n, (w, x) in enumerate(THREE):
                    last = pe.matmul(t, br[:, w, tb, c, :], axr[:, tb % 2, x, :], start=False, stop=(n == 2))
                last.then_inc(filled, 1)

            pe.wait_ge(zeros_ready, 1)
            for (kind, *at), _ in ring:
                if kind == "hid" and at[0] == 0:
                    pe.wait_ge(start_in, 16)
                    pe.matmul(claim("hid", 0)[:, 0:B], first("w0"), first("emb"),
                              start=True, stop=True).then_inc(filled, 1)
                elif kind == "hid":
                    pe.wait_ge(hid_ready, 1)
                    pe.matmul(claim("hid", 1)[:, 0:B], first("w1"), hid_t[:, 0, :],
                              start=True, stop=True).then_inc(filled, 1)
                elif kind == "logit":
                    t = claim("logit")[0:B, 0:KX]
                    pe.wait_ge(hid_ready, 2)
                    pe.wait_ge(memsets, 4)
                    pe.matmul(t, hid_t[:, 1, :], first("w2"), start=True, stop=False)
                    pe.matmul(t, ones[:, :], first("b2", 1), start=False, stop=True).then_inc(filled, 1)
                elif kind == "ctx":
                    pe.matmul(claim("ctx")[:, 0:B], first("cw"), first("emb"),
                              start=True, stop=True).then_inc(filled, 1)
                elif kind == "att":
                    t = claim("att")
                    pe.wait_ge(att_ready, 1)
                    pe.wait_ge(keep_in, 16)
                    for k in range(2):
                        pe.transpose(t[:, k * B:(k + 1) * B], att_wide[:, k * P:(k + 1) * P], ident[0:B, 0:B])
                    pe.transpose(t[0:KX, 2 * B:3 * B], att_wide[:, 0:KX * R:R], ident[0:B, 0:B])\
                      .then_inc(filled, 1)
                elif kind == "zero":
                    spread_zeros(*at)
                elif kind == "agg":
                    aggregate(*at)
                elif kind == "mix":
                    mix(*at)
                elif kind == "gate":
                    project(at[0], 0, at[1])
                elif kind == "up":
                    project(at[0], 1, at[1])
                elif kind == "down":
                    down(*at)
                elif kind == "turn":
                    turn(*at)
                elif kind == "conv":
                    convolve(*at)
                elif kind == "back":
                    turn_back(*at)
                elif kind == "lora_a":
                    gate_a(*at)
                elif kind == "lora_b":
                    gate_b(*at)
                elif kind == "ax":
                    lora_down(*at)
                elif kind == "lin":
                    linear(*at)

        @block.scalar
        def _(act):
            act.dma_start(acc_f[:, 0:START_W], start).then_inc(start_in, 16)
            act.dma_start(kc[:, :], keep).then_inc(keep_in, 16)
            act.wait_ge(start_in, 16)
            for n, b in enumerate(("b0", "b1")):
                is_filled(act, "hid", n)
                act.activation(hid_t[:, n, :], bank("hid", n)[:, 0:B], ACT.Gelu, bias=first(b))\
                   .then_inc(freed["act"], 1)
                act.wait_ge(freed["act"], n + 1)
                act.sem_inc(hid_ready, 1)
            act.wait_ge(negmax_ready, 1)
            act.activation(soft[:, 4:4 + KX], bank("logit")[0:B, 0:KX], ACT.Exp, bias=soft[:, 1:2],
                           accum_out=soft[:, 2:3]).then_inc(freed["act"], 1)
            act.activation(convw[:, 0, :], first("conv"), ACT.Copy).then_inc(conv_hi, 1)

            def bias_hi(tb):
                act.wait_ge(chooser_ready, tb + 1)
                act.wait_ge(memsets, 4)
                if tb:
                    act.wait_ge(filled, place[("mix", tb - 1, G - 1)] + 1)
                act.activation(abr[0:KX, :], abf[:, :], ACT.Copy).then_inc(ab_hi, 1)

            def mixed_hi(tb, c):
                is_filled(act, "mix", tb, c)
                act.activation(mixed_v[:, tb % 2, 0, c, :], bank("mix", tb, c), ACT.Copy).then_inc(mix_hi, 1)

            def silu(u):
                is_freed(act, "gate", u, G - 1)
                g = acc[:, u % 2, 0, :]
                act.activation(g, g, ACT.Silu).then_inc(silu_done, 1)

            def first_group(u, kind):
                name = ("gate", "up")[kind]
                is_filled(act, name, u, 0)
                if u >= 2:
                    act.wait_ge(hid_lo, u - 1)
                act.activation(acc[:, u % 2, kind, :], bank(name, u, 0), ACT.Copy,
                               scale=sgu[:, u % IT, kind, 0:1]).then_inc(freed["act"], 1)

            def product_hi(u):
                act.wait_ge(prod_done, u + 1)
                act.activation(hid[:, u % 2, 0, :], acc[:, u % 2, 1, :], ACT.Copy).then_inc(hid_hi, 1)

            def scale_down(u, c):
                n = u * C + c
                is_filled(act, "down", u, c)
                if n >= 3:
                    act.wait_ge(added, n - 2)
                act.activation(part[:, n % 3, :], bank("down", u, c), ACT.Copy,
                               scale=sd[:, c, u % IT:u % IT + 1]).then_inc(freed["act"], 1)

            bias_hi(0)
            for c in range(G):
                mixed_hi(0, c)
            for u in range(UNITS + 2):
                tb, it = divmod(u, IT)
                if 1 <= u <= UNITS:
                    silu(u - 1)
                if u < UNITS:
                    first_group(u, 0)
                if 1 <= u <= UNITS:
                    product_hi(u - 1)
                if u < UNITS:
                    first_group(u, 1)
                if 1 <= u <= UNITS:
                    for c in range(C):
                        scale_down(u - 1, c)
                if u < UNITS and tb + 1 < TB:
                    if it == MIX_AT - 1:
                        bias_hi(tb + 1)
                    if MIX_AT < it <= MIX_AT + G:
                        mixed_hi(tb + 1, it - MIX_AT - 1)

            def turned_hi(q):
                is_filled(act, "turn", q)
                if q == 0:
                    act.wait_ge(pads, 1)
                act.activation(cin[:, q % 2, 0, :, 1:1 + P],
                               bank("turn", q).rearrange("p (b m) -> p b m", b=QB), ACT.Copy)\
                   .then_inc(turn_hi, 1)

            def back_in_hi(q):
                is_filled(act, "back", q)
                act.activation(lin_in[:, (q // 4) % 2, 0, (q % 4) * QB:(q % 4 + 1) * QB, :, :],
                               bank("back", q).rearrange("p (b k o) -> p b k o", b=QB, k=PH), ACT.Copy)\
                   .then_inc(back_hi, 1)

            is_filled(act, "down", UNITS - 1, C - 1)
            for (kind, *at), _ in ring[place[("turn", 0)]:]:
                if kind == "turn":
                    turned_hi(*at)
                    if at[0] == 1:
                        act.wait_ge(k_in, 16)
                        act.activation(kr[:, 0].rearrange("p k c m -> p (k c m)"), k_f, ACT.Copy)\
                           .then_inc(k_hi, 1)
                        for h in range(TB):
                            last = act.activation(ar[:, 0, :, h, 64:96],
                                                  kept("sha").rearrange("p (k r) -> p k r", k=PH), ACT.Copy)
                        last.then_inc(sh_hi, 1)
                        act.wait_ge(shb_in, 16)
                        for h in range(TB):
                            last = act.activation(br[64:96, 0, h, :, :].rearrange("p c m -> p (c m)"),
                                                  shb_f, ACT.Copy)
                        last.then_inc(sh_hi, 1)
                elif kind == "back":
                    back_in_hi(*at)
                elif kind == "lora_a":
                    is_filled(act, "lora_a", at[0])
                    act.activation(ar[:, 0, at[0], :, 0:64],
                                   bank("lora_a", at[0])[:, 0:GB * R].rearrange("p (t r) -> p t r", t=TB),
                                   ACT.Copy).then_inc(la_hi, 1)
                elif kind == "lora_b":
                    is_filled(act, "lora_b", at[0])
                    for h in range(2):
                        last = act.activation(
                            br[0:64, 0, 2 * at[0] + h, :, :].rearrange("p c m -> p (c m)"),
                            bank("lora_b", at[0])[64 * h:64 * h + 64, :], ACT.Copy)
                    last.then_inc(lb_hi, 1)
                elif kind == "ax":
                    tb = at[0]
                    is_filled(act, "ax", tb)
                    t = bank("ax", tb)
                    act.wait_ge(pads, 3)
                    act.activation(axr[0:32, tb % 2, 0, 0:256], t[0:32, 0:256], ACT.Copy)
                    act.activation(axr[32:64, tb % 2, 0, 256:512], t[32:64, 256:512], ACT.Copy)
                    act.activation(axr[64:96, tb % 2, 0, :], t[64:96, :], ACT.Copy).then_inc(ax_hi, 1)

        @block.gpsimd
        def _(pool):
            pool.memset(ones[:, :], 1.0).then_inc(memsets, 1)
            pool.memset(onesr[:, :].bitcast(F32), 1.0).then_inc(memsets, 1)
            pool.memset(abr[:, :].bitcast(F32), 0.0).then_inc(memsets, 1)
            pool.memset(blocks[:, :, :], 0.0).then_inc(memsets, 1)
            for u in range(UNITS):
                tb = u // IT
                if u % IT == 0:
                    pool.wait_ge(resid_in[tb], 16)
                for c in range(C):
                    n = u * C + c
                    is_freed(pool, "down", u, c)
                    if n >= C:
                        pool.wait_ge(added, n - C + 1)
                    r = resid[:, tb * BB:(tb + 1) * BB, c, :]
                    pool.tensor_tensor(r, r, part[:, n % 3, :].rearrange("p (b o) -> p b o", b=BB),
                                       ALU.add).then_inc(added, 1)
            pool.memset(cin[:, :, :, :, 0:130:129].rearrange("p s h b e -> p (s h b) e").bitcast(F32), 0.0)\
                .then_inc(pads, 1)
            pool.wait_ge(pads, 1)
            pool.memset(axr[0:32, :, :, 256:512].bitcast(F32), 0.0).then_inc(pads, 1)
            pool.wait_ge(pads, 2)
            pool.memset(axr[32:64, :, :, 0:256].bitcast(F32), 0.0).then_inc(pads, 1)

        @block.vector
        def _(dve):
            steps = [0]

            def chain(ins):
                steps[0] += 1
                ins.then_inc(dve_chain, 1)
                dve.wait_ge(dve_chain, steps[0])

            def split_codes(it, kind):
                is_filled(dve, "zero", it, kind)
                dve.wait_ge(codes_in[it % 2], 16 * (it // 2 + 1))
                if it == IT - 1 and kind == 1:
                    is_filled(dve, "zero", IT - 1, 2)
                dst = wgu_v[:, it, kind, :, :] if kind < 2 else wd_v[:, it, :, :]
                dve.tensor_tensor(dst.rearrange("p a b -> p (a b)"),
                                  stage[:, it % 2, kind * 512:(kind + 1) * 512].bitcast(I32),
                                  bank("zero", it, kind), ALU.subtract).then_inc(freed["dve"], 1)

            def choose(tb):
                if tb:
                    is_filled(dve, "agg", tb - 1)
                for k in range(2):
                    a = attrep[:, k, tb * BB:(tb + 1) * BB].unsqueeze(2).to_broadcast([P, BB, S])
                    d = kept("delta").unsqueeze(1).to_broadcast([P, BB, S])
                    dve.tensor_tensor(chooser[:, k, :].rearrange("p (b i) -> p b i", b=BB), a, d, ALU.mult)
                if tb:
                    dve.wait_ge(ab_lo, tb)
                a = att_t[:, tb * BB:(tb + 1) * BB].unsqueeze(2).to_broadcast([KX, BB, S])
                b = kept("bk", KX).unsqueeze(1).to_broadcast([KX, BB, S])
                dve.tensor_tensor(abf[:, :].rearrange("k (b o) -> k b o", b=BB), a, b, ALU.mult)\
                   .then_inc(chooser_ready, 1)

            def bias_lo(tb):
                dve.wait_ge(ab_hi, tb + 1)
                dve.tensor_tensor(abr[32:32 + KX, :], abf[:, :], abr[0:KX, :], ALU.subtract)\
                   .then_inc(ab_lo, 1)

            def place_blocks(tb):
                is_filled(dve, "agg", tb)
                if tb:
                    dve.wait_ge(filled, place[("mix", tb - 1, G - 1)] + 1)
                t = bank("agg", tb)[:, 0:4 * S].rearrange("p (n o) -> p n o", n=4)
                for j in range(4):
                    r = slice(S * j, S * j + S)
                    last = dve.tensor_copy(blocks[r, :, r], t[r])
                last.then_inc(freed["dve"], 1)

            def mixed_lo(tb, c):
                dve.wait_ge(mix_hi, tb * G + c + 1)
                dve.tensor_tensor(mixed_v[:, tb % 2, 1, c, :], bank("mix", tb, c),
                                  mixed_v[:, tb % 2, 0, c, :], ALU.subtract).then_inc(freed["dve"], 1)

            def add_group(u, kind, g):
                name = ("gate", "up")[kind]
                is_filled(dve, name, u, g)
                is_freed(dve, name, u, g - 1)
                a = acc[:, u % 2, kind, :]
                dve.scalar_tensor_tensor(a, bank(name, u, g), sgu[:, u % IT, kind, g:g + 1], a,
                                         ALU.mult, ALU.add).then_inc(freed["dve"], 1)

            def product(u):
                dve.wait_ge(silu_done, u + 1)
                is_freed(dve, "up", u, G - 1)
                dve.tensor_tensor(acc[:, u % 2, 1, :], acc[:, u % 2, 0, :], acc[:, u % 2, 1, :],
                                  ALU.mult).then_inc(prod_done, 1)

            def product_lo(u):
                dve.wait_ge(hid_hi, u + 1)
                dve.tensor_tensor(hid[:, u % 2, 1, :], acc[:, u % 2, 1, :], hid[:, u % 2, 0, :],
                                  ALU.subtract).then_inc(hid_lo, 1)

            dve.wait_ge(zeros_in, 16)
            dve.tensor_copy(zeros_r, zeros_i)
            dve.wait_ge(keep_in, 16)
            dve.tensor_copy(identr[:, :], ident[0:3 * IT, 0:3 * IT]).then_inc(zeros_ready, 1)
            for kind in range(3):
                split_codes(0, kind)
            is_filled(dve, "logit")
            chain(dve.reduce_max(soft[:, 0:1], bank("logit")[0:B, 0:KX], AX.X))
            dve.tensor_scalar(soft[:, 1:2], soft[:, 0:1], -1.0, None, ALU.mult).then_inc(negmax_ready, 1)
            is_filled(dve, "ctx")
            dve.tensor_scalar(ctxb[:, :], bank("ctx")[:, 0:B], first("fside"), None, ALU.add)\
               .then_inc(freed["dve"], 1)
            is_freed(dve, "logit")
            chain(dve.reciprocal(soft[:, 3:4], soft[:, 2:3]))
            dve.tensor_scalar(att_wide.rearrange("b (k i) -> b k i", k=KX),
                              soft[:, 4:4 + KX].unsqueeze(2).to_broadcast([B, KX, R]), soft[:, 3:4], None,
                              ALU.mult).then_inc(att_ready, 1)
            is_filled(dve, "att")
            dve.tensor_copy(attrep[:, :, :].rearrange("p k b -> p (k b)"), bank("att")[:, 0:2 * B])
            dve.tensor_copy(att_t[:, :], bank("att")[0:KX, 2 * B:3 * B]).then_inc(freed["dve"], 1)
            is_freed(dve, "att")
            choose(0)
            dve.wait_ge(memsets, 4)
            bias_lo(0)
            place_blocks(0)
            dve.wait_ge(conv_hi, 1)
            dve.tensor_tensor(convw[:, 1, :], first("conv"), convw[:, 0, :], ALU.subtract).then_inc(conv_lo, 1)
            for c in range(G):
                mixed_lo(0, c)

            for u in range(UNITS + 1):
                tb, it = divmod(u, IT)
                prep = u + 1 < IT
                if u >= 1:
                    product(u - 1)
                if u < UNITS:
                    if prep:
                        split_codes(u + 1, 0)
                    add_group(u, 0, 1)
                if u >= 1:
                    product_lo(u - 1)
                if u < UNITS:
                    add_group(u, 1, 1)
                    if prep:
                        split_codes(u + 1, 1)
                    add_group(u, 0, 2)
                    add_group(u, 1, 2)
                    if prep:
                        split_codes(u + 1, 2)
                    add_group(u, 0, 3)
                    add_group(u, 1, 3)
                if u < UNITS and tb + 1 < TB:
                    if it == MIX_AT - 1:
                        choose(tb + 1)
                        bias_lo(tb + 1)
                    if it == MIX_AT:
                        place_blocks(tb + 1)
                    if MIX_AT < it <= MIX_AT + G:
                        mixed_lo(tb + 1, it - MIX_AT - 1)

            dve.wait_ge(hid_lo, UNITS)
            dve.tensor_tensor(gsel.rearrange("p k (b r) -> p (k b) r", r=R),
                              kept("gate").unsqueeze(2).to_broadcast([P, 4 * GB, R]),
                              kept("delta").unsqueeze(1).to_broadcast([P, 4 * GB, R]), ALU.mult)\
               .then_inc(gsel_ready, 1)
            is_filled(dve, "down", UNITS - 1, C - 1)
            for (kind, *at), _ in ring[place[("turn", 0)]:]:
                if kind == "turn":
                    q = at[0]
                    dve.wait_ge(turn_hi, q + 1)
                    dve.tensor_tensor(cin[:, q % 2, 1, :, 1:1 + P],
                                      bank("turn", q).rearrange("p (b m) -> p b m", b=QB),
                                      cin[:, q % 2, 0, :, 1:1 + P], ALU.subtract).then_inc(freed["dve"], 1)
                    if q == 2:
                        dve.wait_ge(k_hi, 1)
                        dve.tensor_tensor(kr[:, 1].rearrange("p k c m -> p (k c m)"), k_f,
                                          kr[:, 0].rearrange("p k c m -> p (k c m)"), ALU.subtract)\
                           .then_inc(k_lo, 1)
                        dve.wait_ge(sh_hi, 1)
                        for h in range(TB):
                            last = dve.tensor_tensor(ar[:, 1, :, h, 64:96],
                                                     kept("sha").rearrange("p (k r) -> p k r", k=PH),
                                                     ar[:, 0, :, h, 64:96], ALU.subtract)
                        last.then_inc(sh_lo, 1)
                        dve.wait_ge(sh_hi, 2)
                        for h in range(TB):
                            last = dve.tensor_tensor(br[64:96, 1, h, :, :].rearrange("p c m -> p (c m)"),
                                                     shb_f,
                                                     br[64:96, 0, h, :, :].rearrange("p c m -> p (c m)"),
                                                     ALU.subtract)
                        last.then_inc(sh_lo, 1)
                elif kind == "conv":
                    q = at[0]
                    is_filled(dve, "conv", q)
                    dve.tensor_tensor(cout[:, q % 2, :, :],
                                      bank("conv", q).rearrange("p (b m) -> p b m", b=QB),
                                      ctxb[:, q * QB:(q + 1) * QB].unsqueeze(2).to_broadcast([P, QB, P]),
                                      ALU.add).then_inc(freed["dve"], 1)
                elif kind == "back":
                    q = at[0]
                    dve.wait_ge(back_hi, q + 1)
                    rows = slice((q % 4) * QB, (q % 4 + 1) * QB)
                    dve.tensor_tensor(lin_in[:, (q // 4) % 2, 1, rows, :, :],
                                      bank("back", q).rearrange("p (b k o) -> p b k o", b=QB, k=PH),
                                      lin_in[:, (q // 4) % 2, 0, rows, :, :], ALU.subtract)\
                       .then_inc(freed["dve"], 1)
                elif kind == "lora_a":
                    k = at[0]
                    dve.wait_ge(la_hi, k + 1)
                    dve.tensor_tensor(ar[:, 1, k, :, 0:64],
                                      bank("lora_a", k)[:, 0:GB * R].rearrange("p (t r) -> p t r", t=TB),
                                      ar[:, 0, k, :, 0:64], ALU.subtract).then_inc(freed["dve"], 1)
                elif kind == "lora_b":
                    dve.wait_ge(lb_hi, at[0] + 1)
                    for h in range(2):
                        tb = 2 * at[0] + h
                        last = dve.tensor_tensor(br[0:64, 1, tb, :, :].rearrange("p c m -> p (c m)"),
                                                 bank("lora_b", at[0])[64 * h:64 * h + 64, :],
                                                 br[0:64, 0, tb, :, :].rearrange("p c m -> p (c m)"),
                                                 ALU.subtract)
                    last.then_inc(freed["dve"], 1)
                elif kind == "ax":
                    tb = at[0]
                    dve.wait_ge(ax_hi, tb + 1)
                    t = bank("ax", tb)
                    for rows, cols in ((slice(0, 32), slice(0, 256)), (slice(32, 64), slice(256, 512)),
                                       (slice(64, 96), slice(0, 512))):
                        last = dve.tensor_tensor(axr[rows, tb % 2, 1, cols], t[rows, cols],
                                                 axr[rows, tb % 2, 0, cols], ALU.subtract)
                    last.then_inc(freed["dve"], 1)
                elif kind == "lin":
                    tb, c = at
                    n = tb * C + c
                    is_filled(dve, "lin", tb, c)
                    if n < 3:
                        dve.wait_ge(added, UNITS * C)
                    else:
                        dve.wait_ge(stored[n % 3], 16 * (n // 3))
                    dve.scalar_tensor_tensor(staged[:, n % 3, :].rearrange("p (b o) -> p b o", b=BB),
                                             bank("lin", tb, c).rearrange("p (b o) -> p b o", b=BB),
                                             kept("bias")[:, c:c + 1],
                                             resid[:, tb * BB:(tb + 1) * BB, c, :],
                                             ALU.add, ALU.add).then_inc(freed["dve"], 1)


def lay_out(d):
    import numpy as np

    def padded(a, rows=P):
        a = a.reshape(a.shape[0], -1)
        return np.concatenate([a, np.zeros((rows - a.shape[0], a.shape[1]), a.dtype)]) if a.shape[0] < rows else a

    def phase_cols(a):
        return a.reshape(*a.shape[:-1], P, C).swapaxes(-1, -2)

    x = d["x"]
    conv = np.zeros((3, PH, S, PH, S), np.float32)
    w = d["L1_cond_weight"]
    for j in range(3):
        for p in range(PH):
            for p2 in range(PH):
                tap = 4 * (j - 1) + p - p2 + 4
                if 0 <= tap <= 8:
                    for o in range(S):
                        g = o // 8
                        conv[j, p, 8 * g:8 * g + 8, p2, o] = w[o, :, tap]
    start = dict(
        w0=d["L0_cond_W0"], w1=d["L0_cond_W1"], w2=d["L0_cond_W2"], emb=d["cond_128"].T,
        cw=np.tile(d["L1_cond_c_weight"].T, (1, PH)), b0=d["L0_cond_b0"][:, None], b1=d["L0_cond_b1"][:, None],
        fside=np.tile(d["fside_S_0"], PH)[:, None], b2=d["L0_cond_b2"][None, :],
        conv=conv.reshape(3, P, P).transpose(1, 0, 2))
    sgu = np.stack([d["L0_ffn_gate_s"], d["L0_ffn_up_s"]])
    keep = dict(
        ident=np.eye(P, dtype=np.float32), delta=np.tile(np.eye(S, dtype=np.float32), (P // S, 1)),
        wmix=d["L0_cond_weight"][..., 0].reshape(2, 4, S, S).transpose(1, 3, 0, 2),
        gate=np.repeat(d["L1_ffn_gate"].T.reshape(4, 4, 1, GB), R, axis=2).transpose(1, 2, 0, 3).reshape(P, 4 * GB),
        sgu=sgu.reshape(2, G, IT, P).transpose(3, 2, 0, 1),
        sd=phase_cols(d["L0_ffn_down_s"]).transpose(2, 1, 0),
        bias=d["L1_ffn_bias"].reshape(P, C), bk=d["L0_cond_bias_k"],
        sha=d["L1_ffn_lora_A_shared"].T.reshape(P, PH, R))
    keep["wmix"] = keep["wmix"].reshape(P, 2 * S)
    guw = np.stack([d["L0_ffn_gate_w"], d["L0_ffn_up_w"]]).reshape(2, G, P, IT, P).transpose(3, 2, 0, 1, 4)
    dw = phase_cols(d["L0_ffn_down_w"]).reshape(IT, P, 1, C, P)
    codes = np.concatenate([guw, dw], axis=2).reshape(IT, P, 12 * P)
    guz = np.stack([d["L0_ffn_gate_z"], d["L0_ffn_up_z"]]).reshape(2, G, IT, P).transpose(0, 2, 1, 3)
    zeros = np.concatenate([guz.reshape(2 * IT, 512), phase_cols(d["L0_ffn_down_z"]).reshape(IT, 512)])
    k = phase_cols(d["L1_ffn_kernel"]).reshape(P, PH * C * P)
    la = d["L1_ffn_lora_A"].reshape(4, 4 * R, P, PH).transpose(1, 0, 3, 2)
    lb = phase_cols(d["L1_ffn_lora_B"].transpose(0, 2, 1)).reshape(4, 4 * R, H).transpose(1, 0, 2)
    shb = phase_cols(d["L1_ffn_lora_B_shared"].T).reshape(R, H)
    arrays = dict(
        start=np.concatenate([padded(start[n]) for n in START], axis=1),
        keep=np.concatenate([padded(keep[n]) for n in KEEP], axis=1),
        codes=codes, zeros=zeros, x_rows=x.reshape(TB, 4, P, H).transpose(0, 2, 1, 3),
        x_phase=x.reshape(B, S, P, PH).transpose(2, 0, 3, 1), k_raw=k, lora_a=la.reshape(P, 4, H),
        lora_b=lb, shared_b=shb)
    return {n: np.ascontiguousarray(a) for n, a in arrays.items()}


def kernel(**inputs):
    import numpy as np
    from concourse import bacc
    from concourse.bass_utils import run_bass_kernel_spmd

    nc = bacc.Bacc("TRN2", target_bir_lowering=False, num_devices=1)
    arrays = lay_out({n: np.asarray(a) for n, a in inputs.items()})
    args = [nc.dram_tensor(n, a.shape, mybir.dt.from_np(a.dtype), kind="ExternalInput").ap()
            for n, a in arrays.items()]
    out = nc.dram_tensor("out", (TB, C, P, TOK), F32, kind="ExternalOutput").ap()
    ffn_block_kernel(nc, *args, out)
    r = run_bass_kernel_spmd(nc, [arrays], core_ids=[0])
    y = r.results[0]["out"].reshape(TB, C, P, BB, S)
    return np.ascontiguousarray(y.transpose(0, 3, 4, 2, 1)).reshape(B, S, H)
```

```python
from contextlib import ExitStack

import concourse.bass as bass
from concourse import mybir

F32 = mybir.dt.float32
F32R = mybir.dt.float32r
I32 = mybir.dt.int32
ALU = mybir.AluOpType
ACT = mybir.ActivationFunctionType
AX = mybir.AxisListType

P = 128
B, S, H = 64, 32, 512
I = 1792
G = H // P
IT = I // P
TOK = 512
TB = B * S // TOK
BB = TOK // S
UNITS = TB * IT
PH = 4
C = H // P
KX = 8
NL, R = 16, 32
GB = 8
QB = 4
NQ = B // QB
BANKS = 8
LAG = 2
HBUF = LAG + 1
SLOTS = 4
AHEAD = 5
MIX_AT = 8

START = dict(w0=128, emb=B, b0=1, w1=128, b1=1, w2=KX, b2=KX, cw=128, fside=1)
CONV_W = 3 * P
KEEP = dict(ident=128, delta=32, wmix=2 * 32, gate=4 * GB, sgu=IT * 2 * G, sd=C * IT, bias=C, bk=32, sha=PH * R)


def spans(widths):
    at, out = 0, {}
    for name, w in widths.items():
        out[name] = (at, at + w)
        at += w
    return out, at


START_AT, START_W = spans(START)
KEEP_AT, KEEP_W = spans(KEEP)


def ring_order():
    out = []

    def add(engine, *tile):
        out.append((tile, engine))

    def codes(it):
        for kind in range(3):
            add("dve", "zero", it, kind)

    codes(0)
    add("act", "hid", 0)
    add("act", "hid", 1)
    add("act", "logit")
    add("dve", "ctx")
    add("dve", "att")
    add("act", "agg", 0)
    codes(1)
    for c in range(G):
        add("dve", "mix", 0, c)
    for it in range(2, AHEAD):
        add("act", "agg", it - 1)
        codes(it)
    for u in range(UNITS + LAG - 1):
        tb, it = divmod(u, IT)
        for g in range(G):
            prep = u + AHEAD < IT
            if u < UNITS:
                add("act" if g == 0 else "dve", "gate", u, g)
                if g == 2 and tb + 1 < TB and MIX_AT < it <= MIX_AT + G:
                    add("dve", "mix", tb + 1, it - MIX_AT - 1)
                if g == 1 and prep:
                    add("dve", "zero", u + AHEAD, 0)
                add("act" if g == 0 else "dve", "up", u, g)
                if g in (1, 2) and prep:
                    add("dve", "zero", u + AHEAD, g)
            if u >= LAG:
                add("act", "down", u - LAG, g)
    add("dve", "turn", 0)
    for q in range(NQ + 5):
        if q + 1 < NQ:
            add("dve", "turn", q + 1)
        if q < NQ:
            add("dve", "conv", q)
        if q == 0:
            for c in range(C):
                add("act", "down", UNITS - 1, c)
        if 1 <= q <= NQ:
            add("dve", "back", q - 1)
        if 1 <= q <= 2:
            add("dve", "lora_a", 2 * q - 2)
            add("dve", "lora_a", 2 * q - 1)
            add("dve", "lora_b", q - 1)
        if q >= 4 and q % 4 == 0 and q // 4 <= TB:
            add("dve", "ax", q // 4 - 1)
        if q >= 5 and (q - 5) // 4 < TB:
            add("dve", "lin", (q - 5) // 4, (q - 5) % 4)
    return out


def ffn_block_kernel(nc, start, keep, conv, codes, zeros, x_rows, x_phase, k_raw, lora_a, lora_b, shared_b, out):
    ring = ring_order()
    place = {tile: n for n, (tile, _) in enumerate(ring)}
    turns = {"act": 0, "dve": 0}
    freed_at = []
    for _, engine in ring:
        turns[engine] += 1
        freed_at.append((engine, turns[engine]))

    with ExitStack() as ctx:
        def sb(name, shape, dt=F32):
            return ctx.enter_context(nc.sbuf_tensor(name, shape, dt))

        def sem(name):
            return ctx.enter_context(nc.semaphore(name))

        psum = ctx.enter_context(nc.psum_tensor("psum", [P, BANKS, 512], F32))

        wgu = sb("wgu", [P, IT * 2 * G * P], F32R)
        wd = sb("wd", [P, IT * C * P], F32R)
        mixed = sb("mixed", [P, 2, 2, G * TOK], F32R)
        hid = sb("hid", [P, HBUF, 2, TOK], F32R)
        resid = sb("resid", [P, B, PH, S])
        acc = sb("acc", [P, 2, 2, TOK])
        part = sb("part", [P, 3, TOK])
        blocks = sb("blocks", [P, BB // 4, P])
        load = sb("load", [P, 5120])
        agg = sb("agg", [P, TB * 4, S])
        abr = sb("abr", [64, TOK], F32R)
        convw = sb("convw", [P, 2, 3 * P], F32R)
        kc = sb("kc", [P, KEEP_W])
        onesr = sb("onesr", [64, P], F32R)
        identr = sb("identr", [3 * IT, 3 * IT], F32R)
        ones = sb("ones", [1, B])
        attrep = sb("attrep", [P, 2, B])
        att_t = sb("att_t", [KX, B])
        ctxb = sb("ctxb", [P, B])
        soft = sb("soft", [B, 4 + KX])

        def kept(name, rows=P):
            a, b = KEEP_AT[name]
            return kc[0:rows, a:b]

        wgu_v = wgu[:, :].rearrange("p (t k g i) -> p t k g i", t=IT, k=2, g=G)
        wd_v = wd[:, :].rearrange("p (t c m) -> p t c m", t=IT, c=C)
        mixed_v = mixed[:, :, :, :].rearrange("p b h (g t) -> p b h g t", g=G)
        sgu = kept("sgu").rearrange("p (t k g) -> p t k g", t=IT, k=2)
        sd = kept("sd").rearrange("p (c t) -> p c t", c=C)
        ident = kept("ident")
        acc_f = acc[:, :, :, :].rearrange("p a b t -> p (a b t)")

        def first(name, rows=P):
            a, b = START_AT[name]
            return acc_f[0:rows, a:b]
        att_wide = acc_f[0:B, 1024:1280]
        zeros_i = acc_f[0:3 * IT, 1280:1792].bitcast(I32)

        def abf(tb):
            return acc_f[0:KX, 1280:1792] if tb == 0 else load[0:KX, 4096:4608]

        hid_t = acc_f[:, 1792:1920].rearrange("p (n b) -> p n b", n=2)
        zeros_r = wgu_v[0:3 * IT, IT - 1, 1, :, :].rearrange("p g i -> p (g i)")
        stage = load[:, 0:2048].rearrange("p (s n) -> p s n", s=SLOTS)
        xrow = load[:, 2048:4096].rearrange("p (t h) -> p t h", t=4)
        chooser = load[:, 4096:5120].rearrange("p (k n) -> p k n", k=2)
        conv_f = acc_f[:, 512:512 + CONV_W]
        k_f = load[:, 0:2048]
        la_f = load[:, 2048:4096].rearrange("p (k n) -> p k n", k=4)
        lb_f = load[:, 0:2048].rearrange("p (k n) -> p k n", k=4)
        shb_f = blocks[64:96, :, :].rearrange("p a b -> p (a b)")
        kr = wgu[:, 0:4096].rearrange("p (h k c m) -> p h k c m", h=2, k=PH, c=C)
        ar = wgu[:, 4096:7168].rearrange("p (h k t r) -> p h k t r", h=2, k=PH, t=TB)
        br = wgu[0:96, 7168:11264].rearrange("p (h t c m) -> p h t c m", h=2, t=TB, c=C)
        cin = wgu[:, 11264:11264 + 2 * 2 * QB * 130].rearrange("p (s h b m) -> p s h b m", s=2, h=2, b=QB)
        cout = acc_f[:, 0:1024].rearrange("p (s b m) -> p s b m", s=2, b=QB)
        gsel = acc_f[:, 1024:2048].rearrange("p (k n) -> p k n", k=4)
        lin_in = mixed[:, :, :, :].rearrange("p s h (b k o) -> p s h b k o", b=BB, k=PH)
        axr = hid[0:96, :, :, :]
        staged = part

        start_in, keep_in, zeros_in, conv_in = sem("start_in"), sem("keep_in"), sem("zeros_in"), sem("conv_in")
        codes_in = [sem(f"codes_in{s}") for s in range(SLOTS)]
        rows_in = sem("rows_in")
        resid_in = [sem(f"resid_in{t}") for t in range(TB)]
        k_in, la_in, lb_in, shb_in = sem("k_in"), sem("la_in"), sem("lb_in"), sem("shb_in")
        stored = [sem(f"stored{i}") for i in range(3)]
        filled = sem("filled")
        freed = {"act": sem("freed_act"), "dve": sem("freed_dve")}
        memsets = sem("memsets")
        zeros_ready = sem("zeros_ready")
        warm = sem("warm")
        negmax_ready, exp_ready = sem("negmax_ready"), sem("exp_ready")
        dve_chain = sem("dve_chain")
        att_ready = sem("att_ready")
        chooser_ready = sem("chooser_ready")
        abf_ready = sem("abf_ready")
        ab_hi, ab_lo = sem("ab_hi"), sem("ab_lo")
        conv_hi, conv_lo = sem("conv_hi"), sem("conv_lo")
        mix_hi = sem("mix_hi")
        blocks_ready = sem("blocks_ready")
        silu_done, prod_done, hid_hi, hid_lo = sem("silu_done"), sem("prod_done"), sem("hid_hi"), sem("hid_lo")
        added = sem("added")
        k_hi, k_lo = sem("k_hi"), sem("k_lo")
        pads = sem("pads")
        ax_pads = sem("ax_pads")
        turn_hi, back_hi, la_hi, lb_hi, ax_hi = (sem("turn_hi"), sem("back_hi"), sem("la_hi"),
                                                 sem("lb_hi"), sem("ax_hi"))
        sh_hi, sh_lo = sem("sh_hi"), sem("sh_lo")
        gsel_ready = sem("gsel_ready")

        def bank(*tile):
            return psum[:, place[tile] % BANKS, :]

        def is_filled(eng, *tile):
            eng.wait_ge(filled, place[tile] + 1)

        def is_freed(eng, *tile):
            engine, count = freed_at[place[tile]]
            eng.wait_ge(freed[engine], count)

        def choose(eng, tb):
            if tb:
                is_filled(eng, "agg", tb - 1)
            for k in range(2):
                a = attrep[:, k, tb * BB:(tb + 1) * BB].unsqueeze(2).to_broadcast([P, BB, S])
                d = kept("delta").unsqueeze(1).to_broadcast([P, BB, S])
                last = eng.tensor_tensor(chooser[:, k, :].rearrange("p (b i) -> p b i", b=BB), a, d, ALU.mult)
            last.then_inc(chooser_ready, 1)

        block = ctx.enter_context(nc.Block())

        @block.sync
        def _(sp):
            def load_codes(it):
                for n in range(3 * it, 3 * it + 3):
                    if n >= SLOTS:
                        is_freed(sp, "zero", *divmod(n - SLOTS, 3))
                    sp.dma_start(stage[:, n % SLOTS, :].bitcast(I32), codes[n]).then_inc(codes_in[n % SLOTS], 16)

            def load_rows(tb):
                if tb:
                    sp.wait_ge(filled, place[("mix", tb - 1, G - 1)] + 1)
                sp.dma_start(xrow, x_rows[tb]).then_inc(rows_in, 16)

            sp.dma_start(acc_f[:, 0:START_W], start).then_inc(start_in, 16)
            load_codes(0)
            load_rows(0)
            load_codes(1)
            sp.dma_start(conv_f, conv).then_inc(conv_in, 16)
            for it in range(2, IT):
                load_codes(it)
                if it == 4:
                    sp.dma_start(resid[:, 0:BB, :, :], x_phase[:, 0:BB]).then_inc(resid_in[0], 16)
                if it == 9:
                    load_rows(1)
            for tb in range(1, TB):
                sp.dma_start(resid[:, tb * BB:(tb + 1) * BB, :, :],
                             x_phase[:, tb * BB:(tb + 1) * BB]).then_inc(resid_in[tb], 16)
            for tb in range(2, TB):
                load_rows(tb)
            sp.wait_ge(filled, place[("mix", TB - 1, G - 1)] + 1)
            sp.dma_start(k_f, k_raw).then_inc(k_in, 16)
            sp.dma_start(la_f, lora_a).then_inc(la_in, 16)
            sp.dma_start(shb_f, shared_b).then_inc(shb_in, 16)
            sp.wait_ge(k_lo, 1)
            sp.dma_start(lb_f, lora_b).then_inc(lb_in, 16)
            for n in range(TB * C):
                tb, c = divmod(n, C)
                is_freed(sp, "lin", tb, c)
                sp.dma_start(out[tb, c], staged[:, n % 3, :]).then_inc(stored[n % 3], 16)
            for s in range(3):
                sp.wait_ge(stored[s], 16 * len(range(s, TB * C, 3)))

        @block.tensor
        def _(pe):
            def claim(*tile):
                n = place[tile]
                if n >= BANKS:
                    engine, count = freed_at[n - BANKS]
                    pe.wait_ge(freed[engine], count)
                return psum[:, n % BANKS, :]

            def spread_zeros(it, kind):
                t = claim("zero", it, kind)
                r = kind * IT + it
                pe.matmul(t, identr[:, r:r + 1].to_broadcast([3 * IT, P]), zeros_r,
                          start=True, stop=True).then_inc(filled, 1)

            def aggregate(tb):
                t = claim("agg", tb)
                pe.wait_ge(chooser_ready, tb + 1)
                for n in range(4):
                    for k in range(2):
                        last = pe.matmul(t[:, n * S:(n + 1) * S], chooser[:, k, n * P:(n + 1) * P],
                                         kept("wmix").rearrange("p (k o) -> p k o", k=2)[:, k, :],
                                         start=(k == 0), stop=(k == 1))
                last.then_inc(filled, 1)

            def mix(tb, c):
                t = claim("mix", tb, c)
                if c == 0:
                    pe.wait_ge(rows_in, 16 * (tb + 1))
                    pe.wait_ge(ab_lo, tb + 1)
                    pe.wait_ge(blocks_ready, tb + 1)
                pe.matmul(t, onesr[:, :], abr[:, :], start=True, stop=False)
                for n in range(4):
                    last = pe.matmul(t[:, n * P:(n + 1) * P], xrow[:, n, c * P:(c + 1) * P],
                                     blocks[:, n, :], start=False, stop=(n == 3))
                last.then_inc(filled, 1)

            def project(u, kind, g):
                tb, it = divmod(u, IT)
                t = claim(("gate", "up")[kind], u, g)
                if it == 0 and kind == 0:
                    is_freed(pe, "mix", tb, g)
                if tb == 0 and g == 0:
                    is_freed(pe, "zero", it, kind)
                for half in range(2):
                    last = pe.matmul(t, wgu_v[:, it, kind, g, :], mixed_v[:, tb % 2, half, g, :],
                                     start=(half == 0), stop=(half == 1))
                last.then_inc(filled, 1)

            def down(u, c):
                it = u % IT
                t = claim("down", u, c)
                if c == 0:
                    pe.wait_ge(hid_lo, u + 1)
                    if u < IT:
                        is_freed(pe, "zero", it, 2)
                for half in range(2):
                    last = pe.matmul(t, wd_v[:, it, c, :], hid[:, u % HBUF, half, :],
                                     start=(half == 0), stop=(half == 1))
                last.then_inc(filled, 1)

            def turn(q):
                t = claim("turn", q)
                tb = q * QB // BB
                pe.wait_ge(added, (tb + 1) * IT * C)
                for j in range(QB):
                    last = pe.transpose(t[:, j * P:(j + 1) * P],
                                        resid[:, q * QB + j, :, :].rearrange("p k o -> p (k o)"), ident)
                last.then_inc(filled, 1)

            def convolve(q):
                t = claim("conv", q)
                if q == 0:
                    pe.wait_ge(conv_lo, 1)
                is_freed(pe, "turn", q)
                n = 0
                for j in range(3):
                    for w, x in ((0, 0), (0, 1), (1, 0)):
                        last = pe.matmul(t, convw[:, w, j * P:(j + 1) * P], cin[:, q % 2, x, :, j:j + P],
                                         start=(n == 0), stop=(n == 8))
                        n += 1
                last.then_inc(filled, 1)

            def turn_back(q):
                t = claim("back", q)
                is_freed(pe, "conv", q)
                for j in range(QB):
                    last = pe.transpose(t[:, j * P:(j + 1) * P], cout[:, q % 2, j, :], ident)
                last.then_inc(filled, 1)

            def gate_a(k):
                t = claim("lora_a", k)
                if k == 0:
                    pe.wait_ge(gsel_ready, 1)
                    pe.wait_ge(la_in, 16)
                for n in range(4):
                    last = pe.matmul(t[:, 0:GB * R], la_f[:, n, k * P:(k + 1) * P], gsel[:, n, :],
                                     start=(n == 0), stop=(n == 3))
                last.then_inc(filled, 1)

            def gate_b(half):
                t = claim("lora_b", half)
                if half == 0:
                    pe.wait_ge(lb_in, 16)
                for n in range(4):
                    last = pe.matmul(t, gsel[:, n, half * P:(half + 1) * P], lb_f[:, n, :],
                                     start=(n == 0), stop=(n == 3))
                last.then_inc(filled, 1)

            THREE = ((0, 0), (0, 1), (1, 0))

            def lora_down(tb):
                t = claim("ax", tb)
                is_freed(pe, "back", 4 * tb + 3)
                if tb == 0:
                    is_freed(pe, "lora_a", PH - 1)
                    pe.wait_ge(sh_lo, 1)
                n = 0
                for k in range(PH):
                    for w, x in THREE:
                        last = pe.matmul(t[0:96, :], ar[:, w, k, tb, :], lin_in[:, tb % 2, x, :, k, :],
                                         start=(n == 0), stop=(n == 11))
                        n += 1
                last.then_inc(filled, 1)

            def linear(tb, c):
                t = claim("lin", tb, c)
                if tb == 0 and c == 0:
                    pe.wait_ge(k_lo, 1)
                    is_freed(pe, "lora_b", 1)
                    pe.wait_ge(sh_lo, 2)
                n = 0
                for k in range(PH):
                    for w, x in THREE:
                        pe.matmul(t, kr[:, w, k, c, :], lin_in[:, tb % 2, x, :, k, :],
                                  start=(n == 0), stop=False)
                        n += 1
                if c == 0:
                    is_freed(pe, "ax", tb)
                for n, (w, x) in enumerate(THREE):
                    last = pe.matmul(t, br[:, w, tb, c, :], axr[:, tb % 2, x, :], start=False, stop=(n == 2))
                last.then_inc(filled, 1)

            pe.wait_ge(zeros_ready, 1)
            for (kind, *at), _ in ring:
                if kind == "hid" and at[0] == 0:
                    pe.wait_ge(start_in, 16)
                    pe.matmul(claim("hid", 0)[:, 0:B], first("w0"), first("emb"),
                              start=True, stop=True).then_inc(filled, 1)
                elif kind == "hid":
                    is_freed(pe, "hid", 0)
                    pe.matmul(claim("hid", 1)[:, 0:B], first("w1"), hid_t[:, 0, :],
                              start=True, stop=True).then_inc(filled, 1)
                elif kind == "logit":
                    t = claim("logit")[0:B, 0:KX]
                    is_freed(pe, "hid", 1)
                    pe.wait_ge(memsets, 4)
                    pe.matmul(t, hid_t[:, 1, :], first("w2"), start=True, stop=False)
                    pe.matmul(t, ones[:, :], first("b2", 1), start=False, stop=True).then_inc(filled, 1)
                elif kind == "ctx":
                    pe.matmul(claim("ctx")[:, 0:B], first("cw"), first("emb"),
                              start=True, stop=True).then_inc(filled, 1)
                elif kind == "att":
                    t = claim("att")
                    pe.wait_ge(att_ready, 1)
                    pe.wait_ge(keep_in, 16)
                    for k in range(2):
                        pe.transpose(t[:, k * B:(k + 1) * B], att_wide[:, k * P:(k + 1) * P], ident[0:B, 0:B])
                    pe.transpose(t[0:KX, 2 * B:3 * B], att_wide[:, 0:KX * R:R], ident[0:B, 0:B])\
                      .then_inc(filled, 1)
                elif kind == "zero":
                    spread_zeros(*at)
                elif kind == "agg":
                    aggregate(*at)
                elif kind == "mix":
                    mix(*at)
                elif kind == "gate":
                    project(at[0], 0, at[1])
                elif kind == "up":
                    project(at[0], 1, at[1])
                elif kind == "down":
                    down(*at)
                elif kind == "turn":
                    turn(*at)
                elif kind == "conv":
                    convolve(*at)
                elif kind == "back":
                    turn_back(*at)
                elif kind == "lora_a":
                    gate_a(*at)
                elif kind == "lora_b":
                    gate_b(*at)
                elif kind == "ax":
                    lora_down(*at)
                elif kind == "lin":
                    linear(*at)

        @block.scalar
        def _(act):
            act.dma_start(kc[:, :], keep).then_inc(keep_in, 16)
            act.dma_start(zeros_i, zeros).then_inc(zeros_in, 16)
            act.wait_ge(memsets, 1)
            act.activation(soft[0:1, 0:1], ones[0:1, 0:1], ACT.Gelu).then_inc(warm, 1)
            act.wait_ge(start_in, 16)
            for n, b in enumerate(("b0", "b1")):
                is_filled(act, "hid", n)
                act.activation(hid_t[:, n, :], bank("hid", n)[:, 0:B], ACT.Gelu, bias=first(b))\
                   .then_inc(freed["act"], 1)
            act.wait_ge(warm, 1)
            act.activation(soft[0:1, 0:1], ones[0:1, 0:1], ACT.Exp).then_inc(warm, 1)
            act.wait_ge(negmax_ready, 1)
            act.activation(soft[:, 4:4 + KX], bank("logit")[0:B, 0:KX], ACT.Exp, bias=soft[:, 1:2],
                           accum_out=soft[:, 2:3]).then_inc(freed["act"], 1)

            def bias_hi(tb):
                act.wait_ge(abf_ready, tb + 1)
                act.wait_ge(memsets, 4)
                if tb:
                    act.wait_ge(filled, place[("mix", tb - 1, G - 1)] + 1)
                act.activation(abr[0:KX, :], abf(tb), ACT.Copy).then_inc(ab_hi, 1)

            def mixed_hi(tb, c):
                is_filled(act, "mix", tb, c)
                act.activation(mixed_v[:, tb % 2, 0, c, :], bank("mix", tb, c), ACT.Copy).then_inc(mix_hi, 1)

            def silu(u):
                is_freed(act, "gate", u, G - 1)
                g = acc[:, u % 2, 0, :]
                act.activation(g, g, ACT.Silu).then_inc(silu_done, 1)

            def first_group(u, kind):
                name = ("gate", "up")[kind]
                is_filled(act, name, u, 0)
                if u >= 2:
                    act.wait_ge(hid_lo, u - 1)
                act.activation(acc[:, u % 2, kind, :], bank(name, u, 0), ACT.Copy,
                               scale=sgu[:, u % IT, kind, 0:1]).then_inc(freed["act"], 1)

            def product_hi(u):
                act.wait_ge(prod_done, u + 1)
                act.activation(hid[:, u % HBUF, 0, :], acc[:, u % 2, 1, :], ACT.Copy).then_inc(hid_hi, 1)

            def scale_down(u, c):
                n = u * C + c
                is_filled(act, "down", u, c)
                if n >= 3:
                    act.wait_ge(added, n - 2)
                act.activation(part[:, n % 3, :], bank("down", u, c), ACT.Copy,
                               scale=sd[:, c, u % IT:u % IT + 1]).then_inc(freed["act"], 1)

            def keep_blocks(tb):
                is_filled(act, "agg", tb)
                act.activation(agg[:, 4 * tb:4 * tb + 4, :],
                               bank("agg", tb)[:, 0:4 * S].rearrange("p (n o) -> p n o", n=4), ACT.Copy)\
                   .then_inc(freed["act"], 1)

            def place_blocks(tb):
                is_freed(act, "agg", tb)
                if tb:
                    act.wait_ge(filled, place[("mix", tb - 1, G - 1)] + 1)
                for j in range(4):
                    r = slice(S * j, S * j + S)
                    last = act.activation(blocks[r, :, r], agg[r, 4 * tb:4 * tb + 4, :], ACT.Copy)
                last.then_inc(blocks_ready, 1)

            bias_hi(0)
            keep_blocks(0)
            place_blocks(0)
            for c in range(G):
                mixed_hi(0, c)
            act.wait_ge(conv_in, 16)
            act.activation(convw[:, 0, :], conv_f, ACT.Copy).then_inc(conv_hi, 1)
            for tb in range(1, TB):
                keep_blocks(tb)
            for u in range(UNITS + 1):
                tb, it = divmod(u, IT)
                if u < UNITS:
                    first_group(u, 0)
                if 1 <= u <= UNITS:
                    silu(u - 1)
                if u < UNITS:
                    first_group(u, 1)
                if u >= LAG:
                    scale_down(u - LAG, 0)
                if 1 <= u <= UNITS:
                    product_hi(u - 1)
                if tb + 1 < TB and MIX_AT < it <= MIX_AT + G:
                    mixed_hi(tb + 1, it - MIX_AT - 1)
                for c in range(1, C):
                    if u >= LAG:
                        scale_down(u - LAG, c)
                if tb + 1 < TB and it == MIX_AT:
                    place_blocks(tb + 1)
                if tb + 1 < TB and it == MIX_AT - 2:
                    bias_hi(tb + 1)

            def turned_hi(q):
                is_filled(act, "turn", q)
                if q == 0:
                    act.wait_ge(pads, 1)
                act.activation(cin[:, q % 2, 0, :, 1:1 + P],
                               bank("turn", q).rearrange("p (b m) -> p b m", b=QB), ACT.Copy)\
                   .then_inc(turn_hi, 1)

            def back_in_hi(q):
                is_filled(act, "back", q)
                act.activation(lin_in[:, (q // 4) % 2, 0, (q % 4) * QB:(q % 4 + 1) * QB, :, :],
                               bank("back", q).rearrange("p (b k o) -> p b k o", b=QB, k=PH), ACT.Copy)\
                   .then_inc(back_hi, 1)

            for (kind, *at), _ in ring[place[("turn", 0)]:]:
                if kind == "down":
                    scale_down(*at)
                elif kind == "turn":
                    turned_hi(*at)
                    if at[0] == 1:
                        act.wait_ge(k_in, 16)
                        act.activation(kr[:, 0].rearrange("p k c m -> p (k c m)"), k_f, ACT.Copy)\
                           .then_inc(k_hi, 1)
                        for h in range(TB):
                            last = act.activation(ar[:, 0, :, h, 64:96],
                                                  kept("sha").rearrange("p (k r) -> p k r", k=PH), ACT.Copy)
                        last.then_inc(sh_hi, 1)
                        act.wait_ge(shb_in, 16)
                        for h in range(TB):
                            last = act.activation(br[64:96, 0, h, :, :].rearrange("p c m -> p (c m)"),
                                                  shb_f, ACT.Copy)
                        last.then_inc(sh_hi, 1)
                elif kind == "back":
                    back_in_hi(*at)
                elif kind == "lora_a":
                    is_filled(act, "lora_a", at[0])
                    act.activation(ar[:, 0, at[0], :, 0:64],
                                   bank("lora_a", at[0])[:, 0:GB * R].rearrange("p (t r) -> p t r", t=TB),
                                   ACT.Copy).then_inc(la_hi, 1)
                elif kind == "lora_b":
                    is_filled(act, "lora_b", at[0])
                    for h in range(2):
                        last = act.activation(
                            br[0:64, 0, 2 * at[0] + h, :, :].rearrange("p c m -> p (c m)"),
                            bank("lora_b", at[0])[64 * h:64 * h + 64, :], ACT.Copy)
                    last.then_inc(lb_hi, 1)
                elif kind == "ax":
                    tb = at[0]
                    is_filled(act, "ax", tb)
                    t = bank("ax", tb)
                    act.wait_ge(ax_pads, 2)
                    act.activation(axr[0:32, tb % 2, 0, 0:256], t[0:32, 0:256], ACT.Copy)
                    act.activation(axr[32:64, tb % 2, 0, 256:512], t[32:64, 256:512], ACT.Copy)
                    act.activation(axr[64:96, tb % 2, 0, :], t[64:96, :], ACT.Copy).then_inc(ax_hi, 1)

        @block.gpsimd
        def _(pool):
            pool.memset(ones[:, :], 1.0).then_inc(memsets, 1)
            pool.memset(onesr[:, :].bitcast(F32), 1.0).then_inc(memsets, 1)
            pool.memset(abr[:, :].bitcast(F32), 0.0).then_inc(memsets, 1)
            pool.memset(blocks[:, :, :], 0.0).then_inc(memsets, 1)
            is_freed(pool, "att")
            pool.wait_ge(keep_in, 16)
            for tb in range(1, TB):
                choose(pool, tb)
            for u in range(UNITS):
                tb = u // IT
                if u % IT == 0:
                    pool.wait_ge(resid_in[tb], 16)
                for c in range(C):
                    n = u * C + c
                    is_freed(pool, "down", u, c)
                    if n >= C:
                        pool.wait_ge(added, n - C + 1)
                    r = resid[:, tb * BB:(tb + 1) * BB, c, :]
                    pool.tensor_tensor(r, r, part[:, n % 3, :].rearrange("p (b o) -> p b o", b=BB),
                                       ALU.add).then_inc(added, 1)
            pool.wait_ge(added, UNITS * C)
            pool.memset(axr[0:32, :, :, 256:512].bitcast(F32), 0.0).then_inc(ax_pads, 1)
            pool.wait_ge(ax_pads, 1)
            pool.memset(axr[32:64, :, :, 0:256].bitcast(F32), 0.0).then_inc(ax_pads, 1)

        @block.vector
        def _(dve):
            steps = [0]

            def chain(ins):
                steps[0] += 1
                ins.then_inc(dve_chain, 1)
                dve.wait_ge(dve_chain, steps[0])

            def split_codes(it, kind):
                is_filled(dve, "zero", it, kind)
                n = 3 * it + kind
                dve.wait_ge(codes_in[n % SLOTS], 16 * (n // SLOTS + 1))
                if it == IT - 1 and kind == 1:
                    is_filled(dve, "zero", IT - 1, 2)
                dst = wgu_v[:, it, kind, :, :] if kind < 2 else wd_v[:, it, :, :]
                dve.tensor_tensor(dst.rearrange("p a b -> p (a b)"),
                                  stage[:, n % SLOTS, :].bitcast(I32),
                                  bank("zero", it, kind), ALU.subtract).then_inc(freed["dve"], 1)

            def bias(tb):
                if tb == 1:
                    is_filled(dve, "agg", TB - 1)
                if tb:
                    dve.wait_ge(ab_lo, tb)
                a = att_t[:, tb * BB:(tb + 1) * BB].unsqueeze(2).to_broadcast([KX, BB, S])
                b = kept("bk", KX).unsqueeze(1).to_broadcast([KX, BB, S])
                dve.tensor_tensor(abf(tb).rearrange("k (b o) -> k b o", b=BB), a, b, ALU.mult)\
                   .then_inc(abf_ready, 1)

            def bias_lo(tb):
                dve.wait_ge(ab_hi, tb + 1)
                dve.tensor_tensor(abr[32:32 + KX, :], abf(tb), abr[0:KX, :], ALU.subtract)\
                   .then_inc(ab_lo, 1)

            def mixed_lo(tb, c):
                dve.wait_ge(mix_hi, tb * G + c + 1)
                dve.tensor_tensor(mixed_v[:, tb % 2, 1, c, :], bank("mix", tb, c),
                                  mixed_v[:, tb % 2, 0, c, :], ALU.subtract).then_inc(freed["dve"], 1)

            def add_group(u, kind, g):
                name = ("gate", "up")[kind]
                is_filled(dve, name, u, g)
                is_freed(dve, name, u, g - 1)
                a = acc[:, u % 2, kind, :]
                dve.scalar_tensor_tensor(a, bank(name, u, g), sgu[:, u % IT, kind, g:g + 1], a,
                                         ALU.mult, ALU.add).then_inc(freed["dve"], 1)

            def product(u):
                dve.wait_ge(silu_done, u + 1)
                is_freed(dve, "up", u, G - 1)
                dve.tensor_tensor(acc[:, u % 2, 1, :], acc[:, u % 2, 0, :], acc[:, u % 2, 1, :],
                                  ALU.mult).then_inc(prod_done, 1)

            def product_lo(u):
                dve.wait_ge(hid_hi, u + 1)
                dve.tensor_tensor(hid[:, u % HBUF, 1, :], acc[:, u % 2, 1, :], hid[:, u % HBUF, 0, :],
                                  ALU.subtract).then_inc(hid_lo, 1)

            dve.wait_ge(zeros_in, 16)
            dve.tensor_copy(zeros_r, zeros_i)
            dve.wait_ge(keep_in, 16)
            dve.tensor_copy(identr[:, :], ident[0:3 * IT, 0:3 * IT]).then_inc(zeros_ready, 1)
            for kind in range(3):
                split_codes(0, kind)
            is_filled(dve, "logit")
            dve.wait_ge(warm, 2)
            chain(dve.reduce_max(soft[:, 0:1], bank("logit")[0:B, 0:KX], AX.X))
            dve.tensor_scalar(soft[:, 1:2], soft[:, 0:1], -1.0, None, ALU.mult).then_inc(negmax_ready, 1)
            is_filled(dve, "ctx")
            dve.tensor_scalar(ctxb[:, :], bank("ctx")[:, 0:B], first("fside"), None, ALU.add)\
               .then_inc(freed["dve"], 1)
            is_freed(dve, "logit")
            chain(dve.reciprocal(soft[:, 3:4], soft[:, 2:3]))
            dve.tensor_scalar(att_wide.rearrange("b (k i) -> b k i", k=KX),
                              soft[:, 4:4 + KX].unsqueeze(2).to_broadcast([B, KX, R]), soft[:, 3:4], None,
                              ALU.mult).then_inc(att_ready, 1)
            is_filled(dve, "att")
            dve.tensor_copy(attrep[:, :, :].rearrange("p k b -> p (k b)"), bank("att")[:, 0:2 * B])
            dve.tensor_copy(att_t[:, :], bank("att")[0:KX, 2 * B:3 * B]).then_inc(freed["dve"], 1)
            is_freed(dve, "att")
            choose(dve, 0)
            bias(0)
            dve.wait_ge(memsets, 4)
            bias_lo(0)
            for kind in range(3):
                split_codes(1, kind)
            for c in range(G):
                mixed_lo(0, c)
            dve.wait_ge(conv_hi, 1)
            dve.tensor_tensor(convw[:, 1, :], conv_f, convw[:, 0, :], ALU.subtract).then_inc(conv_lo, 1)
            for it in range(2, AHEAD):
                for kind in range(3):
                    split_codes(it, kind)

            for u in range(UNITS + 1):
                tb, it = divmod(u, IT)
                prep = u + AHEAD < IT
                if u < UNITS:
                    add_group(u, 0, 1)
                    if prep:
                        split_codes(u + AHEAD, 0)
                if u >= 1:
                    product(u - 1)
                if u < UNITS:
                    add_group(u, 1, 1)
                    if prep:
                        split_codes(u + AHEAD, 1)
                    add_group(u, 0, 2)
                if u >= 1:
                    product_lo(u - 1)
                if tb + 1 < TB and MIX_AT < it <= MIX_AT + G:
                    mixed_lo(tb + 1, it - MIX_AT - 1)
                if u < UNITS:
                    add_group(u, 1, 2)
                    if prep:
                        split_codes(u + AHEAD, 2)
                    add_group(u, 0, 3)
                    add_group(u, 1, 3)
                if tb + 1 < TB and it == MIX_AT - 2:
                    bias(tb + 1)
                if tb + 1 < TB and it == MIX_AT - 1:
                    bias_lo(tb + 1)
                if u == UNITS - 1:
                    dve.memset(cin[:, :, :, :, 0:130:129].rearrange("p s h b e -> p (s h b) e").bitcast(F32),
                               0.0).then_inc(pads, 1)

            dve.wait_ge(hid_lo, UNITS)
            dve.tensor_tensor(gsel.rearrange("p k (b r) -> p (k b) r", r=R),
                              kept("gate").unsqueeze(2).to_broadcast([P, 4 * GB, R]),
                              kept("delta").unsqueeze(1).to_broadcast([P, 4 * GB, R]), ALU.mult)\
               .then_inc(gsel_ready, 1)
            for (kind, *at), _ in ring[place[("turn", 0)]:]:
                if kind == "turn":
                    q = at[0]
                    dve.wait_ge(turn_hi, q + 1)
                    dve.tensor_tensor(cin[:, q % 2, 1, :, 1:1 + P],
                                      bank("turn", q).rearrange("p (b m) -> p b m", b=QB),
                                      cin[:, q % 2, 0, :, 1:1 + P], ALU.subtract).then_inc(freed["dve"], 1)
                    if q == 2:
                        dve.wait_ge(k_hi, 1)
                        dve.tensor_tensor(kr[:, 1].rearrange("p k c m -> p (k c m)"), k_f,
                                          kr[:, 0].rearrange("p k c m -> p (k c m)"), ALU.subtract)\
                           .then_inc(k_lo, 1)
                        dve.wait_ge(sh_hi, 1)
                        for h in range(TB):
                            last = dve.tensor_tensor(ar[:, 1, :, h, 64:96],
                                                     kept("sha").rearrange("p (k r) -> p k r", k=PH),
                                                     ar[:, 0, :, h, 64:96], ALU.subtract)
                        last.then_inc(sh_lo, 1)
                        dve.wait_ge(sh_hi, 2)
                        for h in range(TB):
                            last = dve.tensor_tensor(br[64:96, 1, h, :, :].rearrange("p c m -> p (c m)"),
                                                     shb_f,
                                                     br[64:96, 0, h, :, :].rearrange("p c m -> p (c m)"),
                                                     ALU.subtract)
                        last.then_inc(sh_lo, 1)
                elif kind == "conv":
                    q = at[0]
                    is_filled(dve, "conv", q)
                    dve.tensor_tensor(cout[:, q % 2, :, :],
                                      bank("conv", q).rearrange("p (b m) -> p b m", b=QB),
                                      ctxb[:, q * QB:(q + 1) * QB].unsqueeze(2).to_broadcast([P, QB, P]),
                                      ALU.add).then_inc(freed["dve"], 1)
                elif kind == "back":
                    q = at[0]
                    dve.wait_ge(back_hi, q + 1)
                    rows = slice((q % 4) * QB, (q % 4 + 1) * QB)
                    dve.tensor_tensor(lin_in[:, (q // 4) % 2, 1, rows, :, :],
                                      bank("back", q).rearrange("p (b k o) -> p b k o", b=QB, k=PH),
                                      lin_in[:, (q // 4) % 2, 0, rows, :, :], ALU.subtract)\
                       .then_inc(freed["dve"], 1)
                elif kind == "lora_a":
                    k = at[0]
                    dve.wait_ge(la_hi, k + 1)
                    dve.tensor_tensor(ar[:, 1, k, :, 0:64],
                                      bank("lora_a", k)[:, 0:GB * R].rearrange("p (t r) -> p t r", t=TB),
                                      ar[:, 0, k, :, 0:64], ALU.subtract).then_inc(freed["dve"], 1)
                elif kind == "lora_b":
                    dve.wait_ge(lb_hi, at[0] + 1)
                    for h in range(2):
                        tb = 2 * at[0] + h
                        last = dve.tensor_tensor(br[0:64, 1, tb, :, :].rearrange("p c m -> p (c m)"),
                                                 bank("lora_b", at[0])[64 * h:64 * h + 64, :],
                                                 br[0:64, 0, tb, :, :].rearrange("p c m -> p (c m)"),
                                                 ALU.subtract)
                    last.then_inc(freed["dve"], 1)
                elif kind == "ax":
                    tb = at[0]
                    dve.wait_ge(ax_hi, tb + 1)
                    t = bank("ax", tb)
                    for rows, cols in ((slice(0, 32), slice(0, 256)), (slice(32, 64), slice(256, 512)),
                                       (slice(64, 96), slice(0, 512))):
                        last = dve.tensor_tensor(axr[rows, tb % 2, 1, cols], t[rows, cols],
                                                 axr[rows, tb % 2, 0, cols], ALU.subtract)
                    last.then_inc(freed["dve"], 1)
                elif kind == "lin":
                    tb, c = at
                    n = tb * C + c
                    is_filled(dve, "lin", tb, c)
                    if n < 3:
                        dve.wait_ge(added, UNITS * C)
                    else:
                        dve.wait_ge(stored[n % 3], 16 * (n // 3))
                    dve.scalar_tensor_tensor(staged[:, n % 3, :].rearrange("p (b o) -> p b o", b=BB),
                                             bank("lin", tb, c).rearrange("p (b o) -> p b o", b=BB),
                                             kept("bias")[:, c:c + 1],
                                             resid[:, tb * BB:(tb + 1) * BB, c, :],
                                             ALU.add, ALU.add).then_inc(freed["dve"], 1)


def lay_out(d):
    import numpy as np

    def padded(a, rows=P):
        a = a.reshape(a.shape[0], -1)
        return np.concatenate([a, np.zeros((rows - a.shape[0], a.shape[1]), a.dtype)]) if a.shape[0] < rows else a

    def phase_cols(a):
        return a.reshape(*a.shape[:-1], P, C).swapaxes(-1, -2)

    x = d["x"]
    conv = np.zeros((3, PH, S, PH, S), np.float32)
    w = d["L1_cond_weight"]
    for j in range(3):
        for p in range(PH):
            for p2 in range(PH):
                tap = 4 * (j - 1) + p - p2 + 4
                if 0 <= tap <= 8:
                    for o in range(S):
                        g = o // 8
                        conv[j, p, 8 * g:8 * g + 8, p2, o] = w[o, :, tap]
    start = dict(
        w0=d["L0_cond_W0"], w1=d["L0_cond_W1"], w2=d["L0_cond_W2"], emb=d["cond_128"].T,
        cw=np.tile(d["L1_cond_c_weight"].T, (1, PH)), b0=d["L0_cond_b0"][:, None], b1=d["L0_cond_b1"][:, None],
        fside=np.tile(d["fside_S_0"], PH)[:, None], b2=d["L0_cond_b2"][None, :])
    sgu = np.stack([d["L0_ffn_gate_s"], d["L0_ffn_up_s"]])
    keep = dict(
        ident=np.eye(P, dtype=np.float32), delta=np.tile(np.eye(S, dtype=np.float32), (P // S, 1)),
        wmix=d["L0_cond_weight"][..., 0].reshape(2, 4, S, S).transpose(1, 3, 0, 2),
        gate=np.repeat(d["L1_ffn_gate"].T.reshape(4, 4, 1, GB), R, axis=2).transpose(1, 2, 0, 3).reshape(P, 4 * GB),
        sgu=sgu.reshape(2, G, IT, P).transpose(3, 2, 0, 1),
        sd=phase_cols(d["L0_ffn_down_s"]).transpose(2, 1, 0),
        bias=d["L1_ffn_bias"].reshape(P, C), bk=d["L0_cond_bias_k"],
        sha=d["L1_ffn_lora_A_shared"].T.reshape(P, PH, R))
    keep["wmix"] = keep["wmix"].reshape(P, 2 * S)
    guw = np.stack([d["L0_ffn_gate_w"], d["L0_ffn_up_w"]]).reshape(2, G, P, IT, P).transpose(3, 2, 0, 1, 4)
    dw = phase_cols(d["L0_ffn_down_w"]).reshape(IT, P, 1, C, P)
    codes = np.concatenate([guw, dw], axis=2).reshape(IT, P, 3, 512).transpose(0, 2, 1, 3).reshape(3 * IT, P, 512)
    guz = np.stack([d["L0_ffn_gate_z"], d["L0_ffn_up_z"]]).reshape(2, G, IT, P).transpose(0, 2, 1, 3)
    zeros = np.concatenate([guz.reshape(2 * IT, 512), phase_cols(d["L0_ffn_down_z"]).reshape(IT, 512)])
    k = phase_cols(d["L1_ffn_kernel"]).reshape(P, PH * C * P)
    la = d["L1_ffn_lora_A"].reshape(4, 4 * R, P, PH).transpose(1, 0, 3, 2)
    lb = phase_cols(d["L1_ffn_lora_B"].transpose(0, 2, 1)).reshape(4, 4 * R, H).transpose(1, 0, 2)
    shb = phase_cols(d["L1_ffn_lora_B_shared"].T).reshape(R, H)
    arrays = dict(
        start=np.concatenate([padded(start[n]) for n in START], axis=1),
        keep=np.concatenate([padded(keep[n]) for n in KEEP], axis=1),
        conv=conv.reshape(3, P, P).transpose(1, 0, 2).reshape(P, CONV_W), codes=codes, zeros=zeros, x_rows=x.reshape(TB, 4, P, H).transpose(0, 2, 1, 3),
        x_phase=x.reshape(B, S, P, PH).transpose(2, 0, 3, 1), k_raw=k, lora_a=la.reshape(P, 4, H),
        lora_b=lb, shared_b=shb)
    return {n: np.ascontiguousarray(a) for n, a in arrays.items()}


def kernel(**inputs):
    import numpy as np
    from concourse import bacc
    from concourse.bass_utils import run_bass_kernel_spmd

    nc = bacc.Bacc("TRN2", target_bir_lowering=False, num_devices=1)
    arrays = lay_out({n: np.asarray(a) for n, a in inputs.items()})
    args = [nc.dram_tensor(n, a.shape, mybir.dt.from_np(a.dtype), kind="ExternalInput").ap()
            for n, a in arrays.items()]
    out = nc.dram_tensor("out", (TB, C, P, TOK), F32, kind="ExternalOutput").ap()
    ffn_block_kernel(nc, *args, out)
    r = run_bass_kernel_spmd(nc, [arrays], core_ids=[0])
    y = r.results[0]["out"].reshape(TB, C, P, BB, S)
    return np.ascontiguousarray(y.transpose(0, 3, 4, 2, 1)).reshape(B, S, H)
```

```python
from contextlib import ExitStack

import concourse.bass as bass
from concourse import mybir

F32 = mybir.dt.float32
F32R = mybir.dt.float32r
I32 = mybir.dt.int32
ALU = mybir.AluOpType
ACT = mybir.ActivationFunctionType
AX = mybir.AxisListType

P = 128
B, S, H = 64, 32, 512
I = 1792
G = H // P
IT = I // P
TOK = 512
TB = B * S // TOK
BB = TOK // S
UNITS = TB * IT
PH = 4
C = H // P
KX = 8
R = 32
GB = 8
QB = 4
NQ = B // QB
BANKS = 8
LAG = 2
HBUF = LAG + 1
SLOTS = 8
AHEAD = 2
CODES_FIRST = 3
MIX_AT = 7

WOVEN = {UNITS - 2: 2, UNITS - 1: 3, UNITS: 3}
LORA_A_AT, LORA_B_AT = (1, 2), (4, 6)

START = dict(w0=128, emb=B, b0=1, w1=128, b1=1, w2=KX, b2=KX, cw=128, fside=1, sel=128, own=B // 4, one=B)
CONV_W = 3 * P
KEEP = dict(ident=128, delta=32, wmix=32 * KX, gate=4 * GB, sgu=IT * 2 * G, sd=C * IT, bias=C, bk=32)


def spans(widths):
    at, out = 0, {}
    for name, w in widths.items():
        out[name] = (at, at + w)
        at += w
    return out, at


START_AT, START_W = spans(START)
KEEP_AT, KEEP_W = spans(KEEP)


def second_layer():
    out = []

    def add(engine, *tile):
        out.append((tile, engine))

    add("dve", "turn", 0)
    for q in range(NQ + 5):
        if q + 1 < NQ:
            add("dve", "turn", q + 1)
        if q < NQ:
            add("dve", "conv", q)
        if 1 <= q <= NQ:
            add("dve", "back", q - 1)
        if q in LORA_A_AT:
            for k in range(2):
                add("dve", "lora_a", 2 * LORA_A_AT.index(q) + k)
        if q in LORA_B_AT:
            add("dve", "lora_b", LORA_B_AT.index(q))
        if q >= 5 and (q - 5) // 4 < TB:
            add("dve", "lin", (q - 5) // 4, (q - 5) % 4)
        if q >= 4 and q % 4 == 0 and q // 4 <= TB:
            add("dve", "ax", q // 4 - 1)
    return out


def ring_order():
    out = []

    def add(engine, *tile):
        out.append((tile, engine))

    def zero(it, kind):
        add("act" if kind == 2 else "dve", "zero", it, kind)

    start_codes = [(it, kind) for it in range(AHEAD) for kind in range(3)]

    def codes(n):
        for _ in range(min(n, len(start_codes))):
            zero(*start_codes.pop(0))

    add("act", "hid", 0)
    add("act", "hid", 1)
    add("act", "logit")
    add("dve", "ctx")
    codes(2)
    add("dve", "att")
    codes(CODES_FIRST)
    for c in range(G):
        add("dve", "mix", 0, c)
        codes(1)
    codes(3 * AHEAD)
    second = second_layer()
    for u in range(UNITS + LAG):
        tb, it = divmod(u, IT)
        for g in range(G):
            prep = u + AHEAD < IT
            if u < UNITS:
                add("act" if g == 0 else "dve", "gate", u, g)
                if g == 2 and tb + 1 < TB and MIX_AT < it <= MIX_AT + G:
                    add("dve", "mix", tb + 1, it - MIX_AT - 1)
                if g == 1 and prep:
                    zero(u + AHEAD, 0)
                add("act" if g == 0 else "dve", "up", u, g)
                if g in (1, 2) and prep:
                    zero(u + AHEAD, g)
            if u >= LAG:
                add("act", "down", u - LAG, g)
        out += [second.pop(0) for _ in range(WOVEN.get(u, 0))]
    return out + second


def ffn_block_kernel(nc, start, keep, conv, codes, zeros, x_rows, x_phase, k_raw, lora_a, lora_b, shared, out):
    ring = ring_order()
    place = {tile: n for n, (tile, _) in enumerate(ring)}
    turns = {"act": 0, "dve": 0}
    freed_at = []
    for _, engine in ring:
        turns[engine] += 1
        freed_at.append((engine, turns[engine]))

    with ExitStack() as ctx:
        def sb(name, shape, dt=F32):
            return ctx.enter_context(nc.sbuf_tensor(name, shape, dt))

        def sem(name):
            return ctx.enter_context(nc.semaphore(name))

        psum = ctx.enter_context(nc.psum_tensor("psum", [P, BANKS, 512], F32))

        wgu = sb("wgu", [P, IT * 2 * G * P], F32R)
        wd = sb("wd", [P, IT * C * P], F32R)
        mixed = sb("mixed", [P, 2, 2, G * TOK], F32R)
        hid = sb("hid", [P, HBUF, 2, TOK], F32R)
        resid = sb("resid", [P, B, PH, S])
        acc = sb("acc", [P, 2, 2, TOK])
        part = sb("part", [P, 3, TOK])
        blocks = sb("blocks", [P, BB // 4, P])
        load = sb("load", [P, 5120])
        agg = sb("agg", [P, TB * 4, S])
        abr = sb("abr", [64, TOK], F32R)
        convw = sb("convw", [P, 2, 3 * P], F32R)
        kc = sb("kc", [P, KEEP_W])
        onesr = sb("onesr", [64, P], F32R)
        identr = sb("identr", [P, P], F32R)
        att_rows = sb("att_rows", [P, B // 4, KX])
        att_t = sb("att_t", [KX, B])
        ctxb = sb("ctxb", [P, B])
        soft = sb("soft", [B, 4 + KX])
        silu_warm = sb("silu_warm", [1, 1])

        def kept(name, rows=P):
            a, b = KEEP_AT[name]
            return kc[0:rows, a:b]

        wgu_v = wgu[:, :].rearrange("p (t k g i) -> p t k g i", t=IT, k=2, g=G)
        wd_v = wd[:, :].rearrange("p (t c m) -> p t c m", t=IT, c=C)
        mixed_v = mixed[:, :, :, :].rearrange("p b h (g t) -> p b h g t", g=G)
        sgu = kept("sgu").rearrange("p (t k g) -> p t k g", t=IT, k=2)
        sd = kept("sd").rearrange("p (c t) -> p c t", c=C)
        ident = kept("ident")
        acc_f = acc[:, :, :, :].rearrange("p a b t -> p (a b t)")

        def first(name, rows=P):
            a, b = START_AT[name]
            return acc_f[0:rows, a:b]
        conv_f = acc_f[:, 704:704 + CONV_W]
        att_own = acc_f[0:B, 1088:1088 + (B // 4) * KX].rearrange("b (n k) -> b n k", k=KX)
        att_n = acc_f[0:B, 1216:1216 + KX]
        zeros_i = acc_f[0:3 * IT, 1536:2048].bitcast(I32)

        def abf(tb):
            return acc_f[0:KX, 1536:2048] if tb == 0 else load[0:KX, 4096:4608]

        hid_t = acc_f[:, 1280:1408].rearrange("p (n b) -> p n b", n=2)
        zeros_r = wgu_v[0:3 * IT, IT - 1, 1, :, :].rearrange("p g i -> p (g i)")
        stages = (load[:, 0:2048].rearrange("p (s n) -> p s n", s=SLOTS // 2),
                  resid[:, B - BB:B, :, :].rearrange("p (s b) k o -> p s (b k o)", s=SLOTS // 2))

        def stage(n):
            half, slot = divmod(n % SLOTS, SLOTS // 2)
            return stages[half][:, slot, :].bitcast(I32)

        xrow = load[:, 2048:4096].rearrange("p (t h) -> p t h", t=4)
        terms = load[:, 4096:5120].rearrange("p (n o k) -> p n o k", n=4, k=KX)
        k_f = load[:, 0:2048]
        la_f = load[:, 2048:4096].rearrange("p (k n) -> p k n", k=4)
        lb_f = la_f
        shared_f = acc_f[:, 0:640]
        shb_f = acc_f[64:96, 0:512]
        sha_f = acc_f[:, 512:640].rearrange("p (k r) -> p k r", k=PH)
        cin = wgu[:, 0:2080].rearrange("p (s h b m) -> p s h b m", s=2, h=2, b=QB)
        kr = wgu[:, 2080:6176].rearrange("p (h k c m) -> p h k c m", h=2, k=PH, c=C)
        ar = wgu[:, 6176:9248].rearrange("p (h k t r) -> p h k t r", h=2, k=PH, t=TB)
        br = wgu[0:96, 9248:13344].rearrange("p (h t c m) -> p h t c m", h=2, t=TB, c=C)
        cout = load[:, 4096:5120].rearrange("p (s b m) -> p s b m", s=2, b=QB)
        gsel_two = (agg[:, :, :].rearrange("p (k b) r -> p k (b r)", k=2),
                    blocks[:, :, :].rearrange("p (k b) r -> p k (b r)", k=2))

        def gsel(n):
            return gsel_two[n // 2][:, n % 2, :]

        lin_in = mixed[:, :, :, :].rearrange("p s h (b k o) -> p s h b k o", b=BB, k=PH)
        axr = hid[0:96, :, :, :]
        staged = part

        start_in, keep_in, zeros_in, conv_in = sem("start_in"), sem("keep_in"), sem("zeros_in"), sem("conv_in")
        codes_in = [sem(f"codes_in{s}") for s in range(SLOTS)]
        rows_in = sem("rows_in")
        resid_in = [sem(f"resid_in{t}") for t in range(TB)]
        k_in, la_in, lb_in, shared_in = sem("k_in"), sem("la_in"), sem("lb_in"), sem("shared_in")
        stored = [sem(f"stored{i}") for i in range(3)]
        filled = sem("filled")
        freed = {"act": sem("freed_act"), "dve": sem("freed_dve")}
        memsets = sem("memsets")
        zeros_ready = sem("zeros_ready")
        down_float = sem("down_float")
        warm = sem("warm")
        negmax_ready, exp_ready = sem("negmax_ready"), sem("exp_ready")
        dve_chain = sem("dve_chain")
        att_ready = sem("att_ready")
        agg_ready = sem("agg_ready")
        pool_chain = sem("pool_chain")
        abf_ready = sem("abf_ready")
        ab_hi, ab_lo = sem("ab_hi"), sem("ab_lo")
        conv_hi, conv_lo = sem("conv_hi"), sem("conv_lo")
        mix_hi = sem("mix_hi")
        blocks_ready = sem("blocks_ready")
        silu_done, prod_done, hid_hi, hid_lo = sem("silu_done"), sem("prod_done"), sem("hid_hi"), sem("hid_lo")
        added = sem("added")
        k_hi, k_lo = sem("k_hi"), sem("k_lo")
        pads = sem("pads")
        ax_pads = sem("ax_pads")
        turn_hi, back_hi, la_hi, lb_hi, ax_hi = (sem("turn_hi"), sem("back_hi"), sem("la_hi"),
                                                 sem("lb_hi"), sem("ax_hi"))
        sh_hi, sh_lo = sem("sh_hi"), sem("sh_lo")
        gsel_ready = sem("gsel_ready")

        def bank(*tile):
            return psum[:, place[tile] % BANKS, :]

        def is_filled(eng, *tile):
            eng.wait_ge(filled, place[tile] + 1)

        def is_freed(eng, *tile):
            engine, count = freed_at[place[tile]]
            eng.wait_ge(freed[engine], count)

        def mixing_terms(eng, tb):
            a = att_rows[:, 4 * tb:4 * tb + 4, :].unsqueeze(2).to_broadcast([P, 4, S, KX])
            w = kept("wmix").rearrange("p (o k) -> p o k", k=KX).unsqueeze(1).to_broadcast([P, 4, S, KX])
            return eng.tensor_tensor(terms, a, w, ALU.mult)

        def bias(eng, tb):
            if tb == 1:
                eng.wait_ge(agg_ready, TB)
            if tb > 1:
                eng.wait_ge(ab_lo, tb)
            a = att_t[:, tb * BB:(tb + 1) * BB].unsqueeze(2).to_broadcast([KX, BB, S])
            b = kept("bk", KX).unsqueeze(1).to_broadcast([KX, BB, S])
            eng.tensor_tensor(abf(tb).rearrange("k (b o) -> k b o", b=BB), a, b, ALU.mult)\
               .then_inc(abf_ready, 1)

        def bias_lo(eng, tb):
            eng.wait_ge(ab_hi, tb + 1)
            eng.tensor_tensor(abr[32:32 + KX, :], abf(tb), abr[0:KX, :], ALU.subtract)\
               .then_inc(ab_lo, 1)

        rest = [tile for tile, _ in second_layer()]
        woven = {u: [rest.pop(0) for _ in range(n)] for u, n in WOVEN.items()}

        block = ctx.enter_context(nc.Block())

        @block.sync
        def _(sp):
            def load_codes(it):
                for n in range(3 * it, 3 * it + 3):
                    if n >= SLOTS:
                        last_it, last_kind = divmod(n - SLOTS, 3)
                        if last_kind == 2:
                            sp.wait_ge(down_float, last_it + 1)
                        else:
                            is_freed(sp, "zero", last_it, last_kind)
                    sp.dma_start(stage(n), codes[n]).then_inc(codes_in[n % SLOTS], 16)

            def load_rows(tb):
                if tb:
                    sp.wait_ge(filled, place[("mix", tb - 1, G - 1)] + 1)
                sp.dma_start(xrow, x_rows[tb]).then_inc(rows_in, 16)

            sp.dma_start(acc_f[:, 0:START_W], start).then_inc(start_in, 16)
            sp.dma_start(kc[:, :], keep).then_inc(keep_in, 16)
            load_codes(0)
            load_rows(0)
            load_codes(1)
            sp.dma_start(conv_f, conv).then_inc(conv_in, 16)
            for it in range(2, IT):
                load_codes(it)
                if it == 4:
                    sp.dma_start(resid[:, 0:BB, :, :], x_phase[:, 0:BB]).then_inc(resid_in[0], 16)
                if it == 9:
                    load_rows(1)
            for tb in range(1, TB):
                if tb == TB - 1:
                    sp.wait_ge(down_float, IT)
                    is_freed(sp, "zero", IT - 1, 1)
                sp.dma_start(resid[:, tb * BB:(tb + 1) * BB, :, :],
                             x_phase[:, tb * BB:(tb + 1) * BB]).then_inc(resid_in[tb], 16)
            for tb in range(2, TB):
                load_rows(tb)
            sp.wait_ge(filled, place[("mix", TB - 1, G - 1)] + 1)
            sp.dma_start(k_f, k_raw).then_inc(k_in, 16)
            sp.dma_start(la_f, lora_a).then_inc(la_in, 16)
            sp.wait_ge(hid_lo, UNITS)
            sp.dma_start(shared_f, shared).then_inc(shared_in, 16)
            is_filled(sp, "lora_a", PH - 1)
            sp.dma_start(lb_f, lora_b).then_inc(lb_in, 16)
            for n in range(TB * C):
                tb, c = divmod(n, C)
                is_freed(sp, "lin", tb, c)
                sp.dma_start(out[tb, c], staged[:, n % 3, :]).then_inc(stored[n % 3], 16)
            for s in range(3):
                sp.wait_ge(stored[s], 16 * len(range(s, TB * C, 3)))

        @block.tensor
        def _(pe):
            def claim(*tile):
                n = place[tile]
                if n >= BANKS:
                    engine, count = freed_at[n - BANKS]
                    pe.wait_ge(freed[engine], count)
                return psum[:, n % BANKS, :]

            def spread_zeros(it, kind):
                t = claim("zero", it, kind)
                if kind == 2:
                    pe.wait_ge(down_float, it + 1)
                    pe.matmul(t, identr[:, :], wd_v[:, it, :, :].rearrange("p a b -> p (a b)"),
                              start=True, stop=False)
                r = kind * IT + it
                pe.matmul(t, identr[0:3 * IT, r:r + 1].to_broadcast([3 * IT, P]), zeros_r,
                          start=(kind < 2), stop=True).then_inc(filled, 1)

            def mix(tb, c):
                t = claim("mix", tb, c)
                if c == 0:
                    if tb == 0:
                        pe.wait_ge(memsets, 3)
                    pe.wait_ge(rows_in, 16 * (tb + 1))
                    pe.wait_ge(ab_lo, tb + 1)
                    pe.wait_ge(blocks_ready, tb + 1)
                pe.matmul(t, onesr[:, :], abr[:, :], start=True, stop=False)
                for n in range(4):
                    last = pe.matmul(t[:, n * P:(n + 1) * P], xrow[:, n, c * P:(c + 1) * P],
                                     blocks[:, n, :], start=False, stop=(n == 3))
                last.then_inc(filled, 1)

            def project(u, kind, g):
                tb, it = divmod(u, IT)
                t = claim(("gate", "up")[kind], u, g)
                if it == 0 and kind == 0:
                    is_freed(pe, "mix", tb, g)
                if tb == 0 and g == 0:
                    is_freed(pe, "zero", it, kind)
                for half in range(2):
                    last = pe.matmul(t, wgu_v[:, it, kind, g, :], mixed_v[:, tb % 2, half, g, :],
                                     start=(half == 0), stop=(half == 1))
                last.then_inc(filled, 1)

            def down(u, c):
                it = u % IT
                t = claim("down", u, c)
                if c == 0:
                    pe.wait_ge(hid_lo, u + 1)
                    if u < IT:
                        is_freed(pe, "zero", it, 2)
                for half in range(2):
                    last = pe.matmul(t, wd_v[:, it, c, :], hid[:, u % HBUF, half, :],
                                     start=(half == 0), stop=(half == 1))
                last.then_inc(filled, 1)

            def turn(q):
                t = claim("turn", q)
                tb = q * QB // BB
                pe.wait_ge(added, (tb + 1) * IT * C)
                for j in range(QB):
                    last = pe.transpose(t[:, j * P:(j + 1) * P],
                                        resid[:, q * QB + j, :, :].rearrange("p k o -> p (k o)"), ident)
                last.then_inc(filled, 1)

            def convolve(q):
                t = claim("conv", q)
                if q == 0:
                    pe.wait_ge(conv_lo, 1)
                is_freed(pe, "turn", q)
                n = 0
                for j in range(3):
                    for w, x in ((0, 0), (0, 1), (1, 0)):
                        last = pe.matmul(t, convw[:, w, j * P:(j + 1) * P], cin[:, q % 2, x, :, j:j + P],
                                         start=(n == 0), stop=(n == 8))
                        n += 1
                last.then_inc(filled, 1)

            def turn_back(q):
                t = claim("back", q)
                is_freed(pe, "conv", q)
                for j in range(QB):
                    last = pe.transpose(t[:, j * P:(j + 1) * P], cout[:, q % 2, j, :], ident)
                last.then_inc(filled, 1)

            def gate_a(k):
                t = claim("lora_a", k)
                if k == 0:
                    pe.wait_ge(gsel_ready, 1)
                    pe.wait_ge(la_in, 16)
                for n in range(4):
                    last = pe.matmul(t[:, 0:GB * R], la_f[:, n, k * P:(k + 1) * P], gsel(n),
                                     start=(n == 0), stop=(n == 3))
                last.then_inc(filled, 1)

            def gate_b(half):
                t = claim("lora_b", half)
                if half == 0:
                    pe.wait_ge(lb_in, 16)
                for n in range(4):
                    last = pe.matmul(t, gsel(n)[:, half * P:(half + 1) * P], lb_f[:, n, :],
                                     start=(n == 0), stop=(n == 3))
                last.then_inc(filled, 1)

            THREE = ((0, 0), (0, 1), (1, 0))

            def lora_down(tb):
                t = claim("ax", tb)
                is_freed(pe, "back", 4 * tb + 3)
                if tb == 0:
                    is_freed(pe, "lora_a", PH - 1)
                    pe.wait_ge(sh_lo, 1)
                n = 0
                for k in range(PH):
                    for w, x in THREE:
                        last = pe.matmul(t[0:96, :], ar[:, w, k, tb, :], lin_in[:, tb % 2, x, :, k, :],
                                         start=(n == 0), stop=(n == 11))
                        n += 1
                last.then_inc(filled, 1)

            def linear(tb, c):
                t = claim("lin", tb, c)
                if tb == 0 and c == 0:
                    pe.wait_ge(k_lo, 1)
                n = 0
                for k in range(PH):
                    for w, x in THREE:
                        pe.matmul(t, kr[:, w, k, c, :], lin_in[:, tb % 2, x, :, k, :],
                                  start=(n == 0), stop=False)
                        n += 1
                if c == 0:
                    is_freed(pe, "ax", tb)
                    is_freed(pe, "lora_b", tb // 2)
                    if tb == 0:
                        pe.wait_ge(sh_lo, 2)
                for n, (w, x) in enumerate(THREE):
                    last = pe.matmul(t, br[:, w, tb, c, :], axr[:, tb % 2, x, :], start=False, stop=(n == 2))
                last.then_inc(filled, 1)

            for (kind, *at), _ in ring:
                if kind == "hid" and at[0] == 0:
                    pe.wait_ge(start_in, 16)
                    pe.matmul(claim("hid", 0)[:, 0:B], first("w0"), first("emb"),
                              start=True, stop=True).then_inc(filled, 1)
                elif kind == "hid":
                    is_freed(pe, "hid", 0)
                    pe.matmul(claim("hid", 1)[:, 0:B], first("w1"), hid_t[:, 0, :],
                              start=True, stop=True).then_inc(filled, 1)
                elif kind == "logit":
                    t = claim("logit")[0:B, 0:KX]
                    is_freed(pe, "hid", 1)
                    pe.matmul(t, hid_t[:, 1, :], first("w2"), start=True, stop=False)
                    pe.matmul(t, first("one", 1), first("b2", 1), start=False, stop=True).then_inc(filled, 1)
                elif kind == "ctx":
                    pe.matmul(claim("ctx")[:, 0:B], first("cw"), first("emb"),
                              start=True, stop=True).then_inc(filled, 1)
                elif kind == "att":
                    t = claim("att")
                    pe.wait_ge(att_ready, 1)
                    pe.wait_ge(keep_in, 16)
                    pe.matmul(t[:, 0:P], first("sel", B), att_own.rearrange("b n k -> b (n k)"),
                              start=True, stop=True)
                    pe.transpose(t[0:KX, P:P + B], att_n, ident[0:B, 0:B]).then_inc(filled, 1)
                elif kind == "zero":
                    if at == [0, 0]:
                        pe.wait_ge(zeros_ready, 1)
                    spread_zeros(*at)
                elif kind == "mix":
                    mix(*at)
                elif kind == "gate":
                    project(at[0], 0, at[1])
                elif kind == "up":
                    project(at[0], 1, at[1])
                elif kind == "down":
                    down(*at)
                elif kind == "turn":
                    turn(*at)
                elif kind == "conv":
                    convolve(*at)
                elif kind == "back":
                    turn_back(*at)
                elif kind == "lora_a":
                    gate_a(*at)
                elif kind == "lora_b":
                    gate_b(*at)
                elif kind == "ax":
                    lora_down(*at)
                elif kind == "lin":
                    linear(*at)

        @block.scalar
        def _(act):
            act.dma_start(zeros_i, zeros).then_inc(zeros_in, 16)
            act.wait_ge(memsets, 1)
            act.activation(soft[0:1, 3:4], blocks[0:1, 0, 0:1], ACT.Gelu).then_inc(warm, 1)
            act.wait_ge(start_in, 16)

            def bias_hi(tb):
                act.wait_ge(abf_ready, tb + 1)
                act.wait_ge(memsets, 3)
                if tb:
                    act.wait_ge(filled, place[("mix", tb - 1, G - 1)] + 1)
                act.activation(abr[0:KX, :], abf(tb), ACT.Copy).then_inc(ab_hi, 1)

            def mixed_hi(tb, c):
                is_filled(act, "mix", tb, c)
                act.activation(mixed_v[:, tb % 2, 0, c, :], bank("mix", tb, c), ACT.Copy).then_inc(mix_hi, 1)

            def silu(u):
                is_freed(act, "gate", u, G - 1)
                g = acc[:, u % 2, 0, :]
                act.activation(g, g, ACT.Silu).then_inc(silu_done, 1)

            def first_group(u, kind):
                name = ("gate", "up")[kind]
                is_filled(act, name, u, 0)
                if u == 0 and kind == 1:
                    act.wait_ge(conv_lo, 1)
                if u >= 2:
                    act.wait_ge(hid_lo, u - 1)
                act.activation(acc[:, u % 2, kind, :], bank(name, u, 0), ACT.Copy,
                               scale=sgu[:, u % IT, kind, 0:1]).then_inc(freed["act"], 1)

            def product_hi(u):
                act.wait_ge(prod_done, u + 1)
                act.activation(hid[:, u % HBUF, 0, :], acc[:, u % 2, 1, :], ACT.Copy).then_inc(hid_hi, 1)

            def scale_down(u, c):
                n = u * C + c
                is_filled(act, "down", u, c)
                if n >= 3:
                    act.wait_ge(added, n - 2)
                act.activation(part[:, n % 3, :], bank("down", u, c), ACT.Copy,
                               scale=sd[:, c, u % IT:u % IT + 1]).then_inc(freed["act"], 1)

            def down_to_float(it):
                n = 3 * it + 2
                act.wait_ge(codes_in[n % SLOTS], 16 * (n // SLOTS + 1))
                act.activation(wd_v[:, it, :, :].rearrange("p a b -> p (a b)"),
                               stage(n), ACT.Copy).then_inc(down_float, 1)

            def keep_down(it):
                is_filled(act, "zero", it, 2)
                act.activation(wd_v[:, it, :, :].rearrange("p a b -> p (a b)"), bank("zero", it, 2),
                               ACT.Copy).then_inc(freed["act"], 1)

            def place_blocks(tb):
                act.wait_ge(agg_ready, tb + 1)
                if tb == 0:
                    act.wait_ge(warm, 3)
                if tb:
                    act.wait_ge(filled, place[("mix", tb - 1, G - 1)] + 1)
                for j in range(4):
                    r = slice(S * j, S * j + S)
                    last = act.activation(blocks[r, :, r], agg[r, 4 * tb:4 * tb + 4, :], ACT.Copy)
                last.then_inc(blocks_ready, 1)

            def turned_hi(q):
                is_filled(act, "turn", q)
                if q == 0:
                    act.wait_ge(pads, 1)
                act.activation(cin[:, q % 2, 0, :, 1:1 + P],
                               bank("turn", q).rearrange("p (b m) -> p b m", b=QB), ACT.Copy)\
                   .then_inc(turn_hi, 1)

            def back_in_hi(q):
                is_filled(act, "back", q)
                act.activation(lin_in[:, (q // 4) % 2, 0, (q % 4) * QB:(q % 4 + 1) * QB, :, :],
                               bank("back", q).rearrange("p (b k o) -> p b k o", b=QB, k=PH), ACT.Copy)\
                   .then_inc(back_hi, 1)

            def second_layer_tile(kind, *at):
                if kind == "turn":
                    turned_hi(*at)
                    if at[0] == 3:
                        act.wait_ge(shared_in, 16)
                        for h in range(TB):
                            last = act.activation(ar[:, 0, :, h, 64:96], sha_f, ACT.Copy)
                        last.then_inc(sh_hi, 1)
                        act.wait_ge(k_in, 16)
                        act.activation(kr[:, 0].rearrange("p k c m -> p (k c m)"), k_f, ACT.Copy)\
                           .then_inc(k_hi, 1)
                    if at[0] == 4:
                        for h in range(TB):
                            last = act.activation(br[64:96, 0, h, :, :].rearrange("p c m -> p (c m)"), shb_f,
                                                  ACT.Copy)
                        last.then_inc(sh_hi, 1)
                elif kind == "back":
                    back_in_hi(*at)
                elif kind == "lora_a":
                    is_filled(act, "lora_a", at[0])
                    act.activation(ar[:, 0, at[0], :, 0:64],
                                   bank("lora_a", at[0])[:, 0:GB * R].rearrange("p (t r) -> p t r", t=TB),
                                   ACT.Copy).then_inc(la_hi, 1)
                elif kind == "lora_b":
                    is_filled(act, "lora_b", at[0])
                    for h in range(2):
                        last = act.activation(
                            br[0:64, 0, 2 * at[0] + h, :, :].rearrange("p c m -> p (c m)"),
                            bank("lora_b", at[0])[64 * h:64 * h + 64, :], ACT.Copy)
                    last.then_inc(lb_hi, 1)
                elif kind == "ax":
                    tb = at[0]
                    is_filled(act, "ax", tb)
                    t = bank("ax", tb)
                    act.wait_ge(ax_pads, 2)
                    act.activation(axr[0:32, tb % 2, 0, 0:256], t[0:32, 0:256], ACT.Copy)
                    act.activation(axr[32:64, tb % 2, 0, 256:512], t[32:64, 256:512], ACT.Copy)
                    act.activation(axr[64:96, tb % 2, 0, :], t[64:96, :], ACT.Copy).then_inc(ax_hi, 1)

            for (kind, *at), _ in ring[:place["gate", 0, 0]]:
                if kind == "hid":
                    is_filled(act, "hid", at[0])
                    act.activation(hid_t[:, at[0], :], bank("hid", at[0])[:, 0:B], ACT.Gelu,
                                   bias=first(("b0", "b1")[at[0]])).then_inc(freed["act"], 1)
                elif kind == "logit":
                    act.wait_ge(warm, 1)
                    act.activation(soft[0:1, 3:4], blocks[0:1, 0, 0:1], ACT.Exp).then_inc(warm, 1)
                    act.wait_ge(negmax_ready, 1)
                    act.activation(soft[:, 4:4 + KX], bank("logit")[0:B, 0:KX], ACT.Exp, bias=soft[:, 1:2],
                                   accum_out=soft[:, 2:3]).then_inc(freed["act"], 1)
                    act.activation(silu_warm[:, :], blocks[0:1, 0, 0:1], ACT.Silu).then_inc(warm, 1)
                elif kind == "zero" and at[1] == 1:
                    down_to_float(at[0])
                elif kind == "zero" and at[1] == 2:
                    keep_down(at[0])
                elif kind == "att":
                    bias_hi(0)
                    place_blocks(0)
                elif kind == "mix":
                    mixed_hi(0, at[1])
            act.wait_ge(conv_in, 16)
            act.activation(convw[:, 0, :], conv_f, ACT.Copy).then_inc(conv_hi, 1)
            for u in range(UNITS + 1):
                tb, it = divmod(u, IT)
                if u < UNITS:
                    first_group(u, 0)
                if 1 <= u <= UNITS:
                    silu(u - 1)
                if u < UNITS:
                    first_group(u, 1)
                if u >= LAG:
                    scale_down(u - LAG, 0)
                if u + AHEAD < IT:
                    down_to_float(u + AHEAD)
                if 1 <= u <= UNITS:
                    product_hi(u - 1)
                if tb + 1 < TB and MIX_AT < it <= MIX_AT + G:
                    mixed_hi(tb + 1, it - MIX_AT - 1)
                for c in range(1, C):
                    if c == 2 and u + AHEAD < IT:
                        keep_down(u + AHEAD)
                    if u >= LAG:
                        scale_down(u - LAG, c)
                if tb + 1 < TB and it == MIX_AT:
                    place_blocks(tb + 1)
                if tb + 1 < TB and it == MIX_AT - 1:
                    bias_hi(tb + 1)
                for tile in woven.get(u, ()):
                    second_layer_tile(*tile)
            for c in range(C):
                scale_down(UNITS - 1, c)
            for tile in rest:
                second_layer_tile(*tile)

        @block.gpsimd
        def _(pool):
            pool.memset(blocks[:, :, :], 0.0).then_inc(memsets, 1)
            pool.memset(onesr[:, :].bitcast(F32), 1.0).then_inc(memsets, 1)
            pool.memset(abr[:, :].bitcast(F32), 0.0).then_inc(memsets, 1)
            is_freed(pool, "att")
            pool.wait_ge(keep_in, 16)
            pool_steps = 0
            pool.wait_ge(memsets, 3)
            bias(pool, 0)
            bias_lo(pool, 0)
            pool.wait_ge(agg_ready, 1)
            pool.wait_ge(ab_lo, 1)
            for tb in range(1, TB):
                ins = mixing_terms(pool, tb)
                for half in (4, 2, 1):
                    pool_steps += 1
                    ins.then_inc(pool_chain, 1)
                    pool.wait_ge(pool_chain, pool_steps)
                    to = terms[:, :, :, 0:half] if half > 1 else agg[:, 4 * tb:4 * tb + 4, :].unsqueeze(3)
                    ins = pool.tensor_tensor(to, terms[:, :, :, 0:half], terms[:, :, :, half:2 * half], ALU.add)
                ins.then_inc(agg_ready, 1)
                pool.wait_ge(agg_ready, tb + 1)
            for (kind, *at), _ in ring:
                if kind == "gate" and at[1] == 0:
                    tb, it = divmod(at[0], IT)
                    if tb + 1 < TB and it == MIX_AT - 2:
                        pool.wait_ge(added, (at[0] - LAG) * C)
                        bias(pool, tb + 1)
                        pool.wait_ge(abf_ready, tb + 2)
                    if tb + 1 < TB and it == MIX_AT:
                        pool.wait_ge(added, (at[0] - LAG) * C)
                        bias_lo(pool, tb + 1)
                        pool.wait_ge(ab_lo, tb + 2)
                elif kind == "down":
                    u, c = at
                    tb = u // IT
                    if u % IT == 0 and c == 0:
                        pool.wait_ge(resid_in[tb], 16)
                    is_freed(pool, "down", u, c)
                    if u:
                        pool.wait_ge(added, (u - 1) * C + c + 1)
                    slot = (u * C + c) % 3
                    r = resid[:, tb * BB:(tb + 1) * BB, c, :]
                    pool.tensor_tensor(r, r, part[:, slot, :].rearrange("p (b o) -> p b o", b=BB),
                                       ALU.add).then_inc(added, 1)
            pool.wait_ge(added, UNITS * C)
            pool.memset(axr[0:32, :, :, 256:512].bitcast(F32), 0.0).then_inc(ax_pads, 1)
            pool.wait_ge(ax_pads, 1)
            pool.memset(axr[32:64, :, :, 0:256].bitcast(F32), 0.0).then_inc(ax_pads, 1)
            pool.wait_ge(ax_pads, 2)
            pool.wait_ge(sh_hi, 1)
            for h in range(TB):
                last = pool.tensor_tensor(ar[:, 1, :, h, 64:96], sha_f,
                                          ar[:, 0, :, h, 64:96], ALU.subtract)
            last.then_inc(sh_lo, 1)
            pool.wait_ge(k_hi, 1)
            pool.tensor_tensor(kr[:, 1].rearrange("p k c m -> p (k c m)"), k_f,
                               kr[:, 0].rearrange("p k c m -> p (k c m)"), ALU.subtract).then_inc(k_lo, 1)
            pool.wait_ge(sh_hi, 2)
            pool.wait_ge(k_lo, 1)
            for h in range(TB):
                last = pool.tensor_tensor(br[64:96, 1, h, :, :].rearrange("p c m -> p (c m)"), shb_f,
                                          br[64:96, 0, h, :, :].rearrange("p c m -> p (c m)"), ALU.subtract)
            last.then_inc(sh_lo, 1)

        @block.vector
        def _(dve):
            steps = [0]

            def chain(ins):
                steps[0] += 1
                ins.then_inc(dve_chain, 1)
                dve.wait_ge(dve_chain, steps[0])

            def split_codes(it, kind):
                is_filled(dve, "zero", it, kind)
                n = 3 * it + kind
                dve.wait_ge(codes_in[n % SLOTS], 16 * (n // SLOTS + 1))
                if it == IT - 1 and kind == 1:
                    is_filled(dve, "zero", IT - 1, 2)
                dve.tensor_tensor(wgu_v[:, it, kind, :, :].rearrange("p a b -> p (a b)"),
                                  stage(n),
                                  bank("zero", it, kind), ALU.add).then_inc(freed["dve"], 1)

            def mixed_lo(tb, c):
                dve.wait_ge(mix_hi, tb * G + c + 1)
                dve.tensor_tensor(mixed_v[:, tb % 2, 1, c, :], bank("mix", tb, c),
                                  mixed_v[:, tb % 2, 0, c, :], ALU.subtract).then_inc(freed["dve"], 1)

            def add_group(u, kind, g):
                name = ("gate", "up")[kind]
                is_filled(dve, name, u, g)
                is_freed(dve, name, u, g - 1)
                a = acc[:, u % 2, kind, :]
                dve.scalar_tensor_tensor(a, bank(name, u, g), sgu[:, u % IT, kind, g:g + 1], a,
                                         ALU.mult, ALU.add).then_inc(freed["dve"], 1)

            def product(u):
                dve.wait_ge(silu_done, u + 1)
                is_freed(dve, "up", u, G - 1)
                dve.tensor_tensor(acc[:, u % 2, 1, :], acc[:, u % 2, 0, :], acc[:, u % 2, 1, :],
                                  ALU.mult).then_inc(prod_done, 1)

            def product_lo(u):
                dve.wait_ge(hid_hi, u + 1)
                dve.tensor_tensor(hid[:, u % HBUF, 1, :], acc[:, u % 2, 1, :], hid[:, u % HBUF, 0, :],
                                  ALU.subtract).then_inc(hid_lo, 1)

            def select_gates():
                for half in range(2):
                    last = dve.tensor_tensor(
                        gsel_two[half].rearrange("p k (b r) -> p (k b) r", r=R),
                        kept("gate")[:, 2 * GB * half:2 * GB * (half + 1)].unsqueeze(2).to_broadcast([P, 2 * GB, R]),
                        kept("delta").unsqueeze(1).to_broadcast([P, 2 * GB, R]), ALU.mult)
                last.then_inc(gsel_ready, 1)

            def second_layer_tile(kind, *at):
                if kind == "turn":
                    q = at[0]
                    if q == 1:
                        select_gates()
                    dve.wait_ge(turn_hi, q + 1)
                    dve.tensor_tensor(cin[:, q % 2, 1, :, 1:1 + P],
                                      bank("turn", q).rearrange("p (b m) -> p b m", b=QB),
                                      cin[:, q % 2, 0, :, 1:1 + P], ALU.subtract).then_inc(freed["dve"], 1)
                elif kind == "conv":
                    q = at[0]
                    is_filled(dve, "conv", q)
                    dve.tensor_tensor(cout[:, q % 2, :, :],
                                      bank("conv", q).rearrange("p (b m) -> p b m", b=QB),
                                      ctxb[:, q * QB:(q + 1) * QB].unsqueeze(2).to_broadcast([P, QB, P]),
                                      ALU.add).then_inc(freed["dve"], 1)
                elif kind == "back":
                    q = at[0]
                    dve.wait_ge(back_hi, q + 1)
                    rows = slice((q % 4) * QB, (q % 4 + 1) * QB)
                    dve.tensor_tensor(lin_in[:, (q // 4) % 2, 1, rows, :, :],
                                      bank("back", q).rearrange("p (b k o) -> p b k o", b=QB, k=PH),
                                      lin_in[:, (q // 4) % 2, 0, rows, :, :], ALU.subtract)\
                       .then_inc(freed["dve"], 1)
                elif kind == "lora_a":
                    k = at[0]
                    dve.wait_ge(la_hi, k + 1)
                    dve.tensor_tensor(ar[:, 1, k, :, 0:64],
                                      bank("lora_a", k)[:, 0:GB * R].rearrange("p (t r) -> p t r", t=TB),
                                      ar[:, 0, k, :, 0:64], ALU.subtract).then_inc(freed["dve"], 1)
                elif kind == "lora_b":
                    dve.wait_ge(lb_hi, at[0] + 1)
                    for h in range(2):
                        tb = 2 * at[0] + h
                        last = dve.tensor_tensor(br[0:64, 1, tb, :, :].rearrange("p c m -> p (c m)"),
                                                 bank("lora_b", at[0])[64 * h:64 * h + 64, :],
                                                 br[0:64, 0, tb, :, :].rearrange("p c m -> p (c m)"),
                                                 ALU.subtract)
                    last.then_inc(freed["dve"], 1)
                elif kind == "ax":
                    tb = at[0]
                    dve.wait_ge(ax_hi, tb + 1)
                    t = bank("ax", tb)
                    for rows, cols in ((slice(0, 32), slice(0, 256)), (slice(32, 64), slice(256, 512)),
                                       (slice(64, 96), slice(0, 512))):
                        last = dve.tensor_tensor(axr[rows, tb % 2, 1, cols], t[rows, cols],
                                                 axr[rows, tb % 2, 0, cols], ALU.subtract)
                    last.then_inc(freed["dve"], 1)
                elif kind == "lin":
                    tb, c = at
                    n = tb * C + c
                    is_filled(dve, "lin", tb, c)
                    if n < 3:
                        dve.wait_ge(added, UNITS * C)
                    else:
                        dve.wait_ge(stored[n % 3], 16 * (n // 3))
                    dve.scalar_tensor_tensor(staged[:, n % 3, :].rearrange("p (b o) -> p b o", b=BB),
                                             bank("lin", tb, c).rearrange("p (b o) -> p b o", b=BB),
                                             kept("bias")[:, c:c + 1],
                                             resid[:, tb * BB:(tb + 1) * BB, c, :],
                                             ALU.add, ALU.add).then_inc(freed["dve"], 1)

            dve.wait_ge(zeros_in, 16)
            dve.tensor_scalar(zeros_r, zeros_i, -1.0, None, ALU.mult)
            dve.wait_ge(keep_in, 16)
            dve.tensor_copy(identr[:, :], ident).then_inc(zeros_ready, 1)
            for (kind, *at), _ in ring[:place["gate", 0, 0]]:
                if kind == "zero" and at[1] < 2:
                    split_codes(*at)
                elif kind == "logit":
                    is_filled(dve, "logit")
                    chain(dve.reduce_max(soft[:, 0:1], bank("logit")[0:B, 0:KX], AX.X))
                    dve.tensor_scalar(soft[:, 1:2], soft[:, 0:1], -1.0, None, ALU.mult).then_inc(negmax_ready, 1)
                elif kind == "ctx":
                    is_filled(dve, "ctx")
                    dve.tensor_scalar(ctxb[:, :], bank("ctx")[:, 0:B], first("fside"), None, ALU.add)\
                       .then_inc(freed["dve"], 1)
                elif kind == "att":
                    is_freed(dve, "logit")
                    chain(dve.reciprocal(soft[:, 3:4], soft[:, 2:3]))
                    dve.scalar_tensor_tensor(
                        att_own, soft[:, 4:4 + KX].unsqueeze(1).to_broadcast([B, B // 4, KX]), soft[:, 3:4],
                        first("own", B).unsqueeze(2).to_broadcast([B, B // 4, KX]), ALU.mult, ALU.mult)
                    dve.tensor_scalar(att_n, soft[:, 4:4 + KX], soft[:, 3:4], None, ALU.mult)\
                       .then_inc(att_ready, 1)
                    is_filled(dve, "att")
                    dve.tensor_copy(att_t[:, :], bank("att")[0:KX, P:P + B])
                    dve.tensor_copy(att_rows[:, :, :].rearrange("p n k -> p (n k)"), bank("att")[:, 0:P])\
                       .then_inc(freed["dve"], 1)
                    is_freed(dve, "att")
                    chain(mixing_terms(dve, 0))
                    dve.tensor_reduce(agg[:, 0:4, :], terms, AX.X, ALU.add).then_inc(agg_ready, 1)
                elif kind == "mix":
                    mixed_lo(0, at[1])
            dve.wait_ge(conv_hi, 1)
            dve.tensor_tensor(convw[:, 1, :], conv_f, convw[:, 0, :], ALU.subtract).then_inc(conv_lo, 1)

            for u in range(UNITS + 1):
                tb, it = divmod(u, IT)
                prep = u + AHEAD < IT
                if u < UNITS:
                    add_group(u, 0, 1)
                    if prep:
                        split_codes(u + AHEAD, 0)
                if u >= 1:
                    product(u - 1)
                if u < UNITS:
                    add_group(u, 1, 1)
                    if prep:
                        split_codes(u + AHEAD, 1)
                    add_group(u, 0, 2)
                if u >= 1:
                    product_lo(u - 1)
                if tb + 1 < TB and MIX_AT < it <= MIX_AT + G:
                    mixed_lo(tb + 1, it - MIX_AT - 1)
                if u < UNITS:
                    add_group(u, 1, 2)
                    add_group(u, 0, 3)
                    add_group(u, 1, 3)
                if u == UNITS - 4:
                    dve.memset(cin[:, :, :, :, 0:130:129].rearrange("p s h b e -> p (s h b) e").bitcast(F32),
                               0.0).then_inc(pads, 1)
                for tile in woven.get(u, ()):
                    second_layer_tile(*tile)
            for tile in rest:
                second_layer_tile(*tile)



def lay_out(d):
    import numpy as np

    def padded(a, rows=P):
        a = a.reshape(a.shape[0], -1)
        return np.concatenate([a, np.zeros((rows - a.shape[0], a.shape[1]), a.dtype)]) if a.shape[0] < rows else a

    def phase_cols(a):
        return a.reshape(*a.shape[:-1], P, C).swapaxes(-1, -2)

    x = d["x"]
    conv = np.zeros((3, PH, S, PH, S), np.float32)
    w = d["L1_cond_weight"]
    for j in range(3):
        for p in range(PH):
            for p2 in range(PH):
                tap = 4 * (j - 1) + p - p2 + 4
                if 0 <= tap <= 8:
                    for o in range(S):
                        g = o // 8
                        conv[j, p, 8 * g:8 * g + 8, p2, o] = w[o, :, tap]
    start = dict(
        w0=d["L0_cond_W0"], w1=d["L0_cond_W1"], w2=d["L0_cond_W2"], emb=d["cond_128"].T,
        cw=np.tile(d["L1_cond_c_weight"].T, (1, PH)), b0=d["L0_cond_b0"][:, None], b1=d["L0_cond_b1"][:, None],
        fside=np.tile(d["fside_S_0"], PH)[:, None], b2=d["L0_cond_b2"][None, :], one=np.ones((1, B), np.float32),
        sel=np.repeat(np.tile(np.eye(4, dtype=np.float32), (B // 4, 1)), S, axis=1),
        own=np.repeat(np.eye(B // 4, dtype=np.float32), 4, axis=0))
    sgu = np.stack([d["L0_ffn_gate_s"], d["L0_ffn_up_s"]])
    keep = dict(
        ident=np.eye(P, dtype=np.float32), delta=np.tile(np.eye(S, dtype=np.float32), (P // S, 1)),
        wmix=np.tile(d["L0_cond_weight"][..., 0].transpose(2, 1, 0), (P // S, 1, 1)),
        gate=np.repeat(d["L1_ffn_gate"].T.reshape(4, 4, 1, GB), R, axis=2).transpose(1, 2, 0, 3).reshape(P, 4 * GB),
        sgu=sgu.reshape(2, G, IT, P).transpose(3, 2, 0, 1),
        sd=phase_cols(d["L0_ffn_down_s"]).transpose(2, 1, 0),
        bias=d["L1_ffn_bias"].reshape(P, C), bk=d["L0_cond_bias_k"])
    guw = np.stack([d["L0_ffn_gate_w"], d["L0_ffn_up_w"]]).reshape(2, G, P, IT, P).transpose(3, 2, 0, 1, 4)
    dw = phase_cols(d["L0_ffn_down_w"]).reshape(IT, P, 1, C, P)
    codes = np.concatenate([guw, dw], axis=2).reshape(IT, P, 3, 512).transpose(0, 2, 1, 3).reshape(3 * IT, P, 512)
    guz = np.stack([d["L0_ffn_gate_z"], d["L0_ffn_up_z"]]).reshape(2, G, IT, P).transpose(0, 2, 1, 3)
    zeros = np.concatenate([guz.reshape(2 * IT, 512), phase_cols(d["L0_ffn_down_z"]).reshape(IT, 512)])
    k = phase_cols(d["L1_ffn_kernel"]).reshape(P, PH * C * P)
    la = d["L1_ffn_lora_A"].reshape(4, 4 * R, P, PH).transpose(1, 0, 3, 2)
    lb = phase_cols(d["L1_ffn_lora_B"].transpose(0, 2, 1)).reshape(4, 4 * R, H).transpose(1, 0, 2)
    shared = np.zeros((P, H + PH * R), np.float32)
    shared[64:96, 0:H] = phase_cols(d["L1_ffn_lora_B_shared"].T).reshape(R, H)
    shared[:, H:] = d["L1_ffn_lora_A_shared"].T.reshape(P, PH * R)
    arrays = dict(
        start=np.concatenate([padded(start[n]) for n in START], axis=1),
        keep=np.concatenate([padded(keep[n]) for n in KEEP], axis=1),
        conv=conv.reshape(3, P, P).transpose(1, 0, 2).reshape(P, CONV_W),
        codes=codes, zeros=zeros, x_rows=x.reshape(TB, 4, P, H).transpose(0, 2, 1, 3),
        x_phase=x.reshape(B, S, P, PH).transpose(2, 0, 3, 1), k_raw=k, lora_a=la.reshape(P, 4, H),
        lora_b=lb, shared=shared)
    return {n: np.ascontiguousarray(a) for n, a in arrays.items()}


def kernel(**inputs):
    import numpy as np
    from concourse import bacc
    from concourse.bass_utils import run_bass_kernel_spmd

    nc = bacc.Bacc("TRN2", target_bir_lowering=False, num_devices=1)
    arrays = lay_out({n: np.asarray(a) for n, a in inputs.items()})
    args = [nc.dram_tensor(n, a.shape, mybir.dt.from_np(a.dtype), kind="ExternalInput").ap()
            for n, a in arrays.items()]
    out = nc.dram_tensor("out", (TB, C, P, TOK), F32, kind="ExternalOutput").ap()
    ffn_block_kernel(nc, *args, out)
    r = run_bass_kernel_spmd(nc, [arrays], core_ids=[0])
    y = r.results[0]["out"].reshape(TB, C, P, BB, S)
    return np.ascontiguousarray(y.transpose(0, 3, 4, 2, 1)).reshape(B, S, H)
```
